# Optimizing a Trainium2 kernel written in Bass

```python
import numpy as np
import jax
import jax.numpy as jnp

def _softmax(x, axis=-1):
    return jax.nn.softmax(x, axis=axis)

def _gelu(x):
    return jax.nn.gelu(x, approximate=True)

def _silu(x):
    return jax.nn.silu(x)

def _sigmoid(x):
    return jax.nn.sigmoid(x)

def _layernorm(x, axis=-1, eps=1e-05):
    m = jnp.mean(x, axis=axis, keepdims=True)
    v = jnp.var(x, axis=axis, keepdims=True)
    return (x - m) / jnp.sqrt(v + eps)

def _scatter_add(tgt, idx, src, axis=0):
    return tgt.at[idx].add(src)

def _segment_sum(src, seg, n):
    return jax.ops.segment_sum(src, seg, n)
kernel_name = 'mk_seq_postln_d1_jaxref_r4_7b5d95'

def setup_inputs(seed: int=0):
    np.random.seed(seed)
    _w = jnp.asarray

    def _L0_attn_setup():
        import jax, jax.numpy as jnp
        import numpy as np
        D_MODEL = 256
        D_STATE = 16
        D_CONV = 4
        EXPAND = 2
        MLP_EXPAND = 2
        D_INNER = EXPAND * D_MODEL
        DT_RANK = (D_MODEL + 15) // 16
        BATCH, SEQ = (2, 256)

        def _layernorm(x, g, b, eps=1e-05):
            m = jnp.mean(x, axis=-1, keepdims=True)
            v = jnp.var(x, axis=-1, keepdims=True)
            return (x - m) * jax.lax.rsqrt(v + eps) * g + b

        def _silu(x):
            return x * jax.nn.sigmoid(x)

        def _mamba(x, in_proj_w, conv_w, conv_b, x_proj_w, dt_proj_w, dt_proj_b, A_log, D_param, out_proj_w):
            xz = x @ in_proj_w.T
            xc, z = jnp.split(xz, 2, axis=-1)
            xc_t = xc.transpose(0, 2, 1)
            xc_t = jax.lax.conv_general_dilated(xc_t, conv_w, window_strides=(1,), padding=[(D_CONV - 1, 0)], dimension_numbers=('NCH', 'OIH', 'NCH'), feature_group_count=D_INNER) + conv_b[None, :, None]
            xc = _silu(xc_t).transpose(0, 2, 1)
            dbc = xc @ x_proj_w.T
            dt, Bm, Cm = jnp.split(dbc, [DT_RANK, DT_RANK + D_STATE], axis=-1)
            dt = jax.nn.softplus(dt @ dt_proj_w.T + dt_proj_b)
            A = -jnp.exp(A_log)

            def step(h, inp):
                dt_t, B_t, C_t, x_t = inp
                dA = jnp.exp(dt_t[..., None] * A)
                h = dA * h + (dt_t * x_t)[..., None] * B_t[:, None, :]
                y = jnp.einsum('bdn,bn->bd', h, C_t)
                return (h, y)
            h0 = jnp.zeros((x.shape[0], D_INNER, D_STATE), x.dtype)
            xs = (dt.transpose(1, 0, 2), Bm.transpose(1, 0, 2), Cm.transpose(1, 0, 2), xc.transpose(1, 0, 2))
            _, ys = jax.lax.scan(step, h0, xs)
            y = ys.transpose(1, 0, 2) + xc * D_param
            y = y * _silu(z)
            return y @ out_proj_w.T
        key = jax.random.key(seed)
        ks = jax.random.split(key, 16)
        s = 0.02
        inp = {'x': jax.random.normal(ks[0], (BATCH, SEQ, D_MODEL), jnp.float32), 'norm1_g': jnp.ones((D_MODEL,), jnp.float32), 'norm1_b': jnp.zeros((D_MODEL,), jnp.float32), 'in_proj_w': jax.random.normal(ks[1], (2 * D_INNER, D_MODEL), jnp.float32) * s, 'conv_w': jax.random.normal(ks[2], (D_INNER, 1, D_CONV), jnp.float32) * s, 'conv_b': jnp.zeros((D_INNER,), jnp.float32), 'x_proj_w': jax.random.normal(ks[3], (DT_RANK + 2 * D_STATE, D_INNER), jnp.float32) * s, 'dt_proj_w': jax.random.normal(ks[4], (D_INNER, DT_RANK), jnp.float32) * s, 'dt_proj_b': jax.random.normal(ks[5], (D_INNER,), jnp.float32) * 0.1, 'A_log': jnp.log(jnp.broadcast_to(jnp.arange(1, D_STATE + 1, dtype=jnp.float32), (D_INNER, D_STATE))), 'D_param': jnp.ones((D_INNER,), jnp.float32), 'out_proj_w': jax.random.normal(ks[6], (D_MODEL, D_INNER), jnp.float32) * s, 'norm2_g': jnp.ones((D_MODEL,), jnp.float32), 'norm2_b': jnp.zeros((D_MODEL,), jnp.float32), 'mlp_w1': jax.random.normal(ks[7], (MLP_EXPAND * D_MODEL, D_MODEL), jnp.float32) * s, 'mlp_b1': jnp.zeros((MLP_EXPAND * D_MODEL,), jnp.float32), 'mlp_w2': jax.random.normal(ks[8], (D_MODEL, MLP_EXPAND * D_MODEL), jnp.float32) * s, 'mlp_b2': jnp.zeros((D_MODEL,), jnp.float32)}
        return inp
    _L0_attn_in = _L0_attn_setup()

    def _L0_ffn_setup():
        import jax, jax.numpy as jnp
        import numpy as np
        DIM = 256
        INTER = 128
        E = 8
        TOP_K = 2
        ROUTE_SCALE = 1.0
        key = jax.random.key(seed)
        ks = jax.random.split(key, 8)
        s_d = 1.0 / np.sqrt(DIM)
        s_f = 1.0 / np.sqrt(INTER)
        x = jax.random.normal(ks[0], (2, 512, DIM), dtype=jnp.float32)
        gate_w = jax.random.uniform(ks[1], (E, DIM), jnp.float32, -s_d, s_d)
        wg = jax.random.uniform(ks[2], (E, INTER, DIM), jnp.float32, -s_d, s_d)
        wu = jax.random.uniform(ks[3], (E, INTER, DIM), jnp.float32, -s_d, s_d)
        wd = jax.random.uniform(ks[4], (E, DIM, INTER), jnp.float32, -s_f, s_f)
        sg = jax.random.uniform(ks[5], (INTER, DIM), jnp.float32, -s_d, s_d)
        su = jax.random.uniform(ks[6], (INTER, DIM), jnp.float32, -s_d, s_d)
        sd = jax.random.uniform(ks[7], (DIM, INTER), jnp.float32, -s_f, s_f)
        return {'x': x, 'gate_w': gate_w, 'wg': wg, 'wu': wu, 'wd': wd, 'sg': sg, 'su': su, 'sd': sd}
    _L0_ffn_in = _L0_ffn_setup()
    _d = {'L0_attn_x': _L0_attn_in['x'], 'L0_attn_norm1_g': _L0_attn_in['norm1_g'], 'L0_attn_norm1_b': _L0_attn_in['norm1_b'], 'L0_attn_in_proj_w': _L0_attn_in['in_proj_w'], 'L0_attn_conv_w': _L0_attn_in['conv_w'], 'L0_attn_conv_b': _L0_attn_in['conv_b'], 'L0_attn_x_proj_w': _L0_attn_in['x_proj_w'], 'L0_attn_dt_proj_w': _L0_attn_in['dt_proj_w'], 'L0_attn_dt_proj_b': _L0_attn_in['dt_proj_b'], 'L0_attn_A_log': _L0_attn_in['A_log'], 'L0_attn_D_param': _L0_attn_in['D_param'], 'L0_attn_out_proj_w': _L0_attn_in['out_proj_w'], 'L0_attn_norm2_g': _L0_attn_in['norm2_g'], 'L0_attn_norm2_b': _L0_attn_in['norm2_b'], 'L0_attn_mlp_w1': _L0_attn_in['mlp_w1'], 'L0_attn_mlp_b1': _L0_attn_in['mlp_b1'], 'L0_attn_mlp_w2': _L0_attn_in['mlp_w2'], 'L0_attn_mlp_b2': _L0_attn_in['mlp_b2'], 'L0_ffn_gate_w': _L0_ffn_in['gate_w'], 'L0_ffn_wg': _L0_ffn_in['wg'], 'L0_ffn_wu': _L0_ffn_in['wu'], 'L0_ffn_wd': _L0_ffn_in['wd'], 'L0_ffn_sg': _L0_ffn_in['sg'], 'L0_ffn_su': _L0_ffn_in['su'], 'L0_ffn_sd': _L0_ffn_in['sd']}
    _x0 = _d['L0_attn_x']
    _d['L0_attn_x'] = jax.random.normal(jax.random.fold_in(jax.random.key(seed), 1), (32, 512, 256), dtype=_x0.dtype)
    del _x0
    return _d

def reference(L0_attn_x, L0_attn_norm1_g, L0_attn_norm1_b, L0_attn_in_proj_w, L0_attn_conv_w, L0_attn_conv_b, L0_attn_x_proj_w, L0_attn_dt_proj_w, L0_attn_dt_proj_b, L0_attn_A_log, L0_attn_D_param, L0_attn_out_proj_w, L0_attn_norm2_g, L0_attn_norm2_b, L0_attn_mlp_w1, L0_attn_mlp_b1, L0_attn_mlp_w2, L0_attn_mlp_b2, L0_ffn_gate_w, L0_ffn_wg, L0_ffn_wu, L0_ffn_wd, L0_ffn_sg, L0_ffn_su, L0_ffn_sd):

    def _L0_attn_ref(x, norm1_g, norm1_b, in_proj_w, conv_w, conv_b, x_proj_w, dt_proj_w, dt_proj_b, A_log, D_param, out_proj_w, norm2_g, norm2_b, mlp_w1, mlp_b1, mlp_w2, mlp_b2):
        import jax, jax.numpy as jnp
        import numpy as np
        D_MODEL = 256
        D_STATE = 16
        D_CONV = 4
        EXPAND = 2
        MLP_EXPAND = 2
        D_INNER = EXPAND * D_MODEL
        DT_RANK = (D_MODEL + 15) // 16
        BATCH, SEQ = (2, 256)

        def _layernorm(x, g, b, eps=1e-05):
            m = jnp.mean(x, axis=-1, keepdims=True)
            v = jnp.var(x, axis=-1, keepdims=True)
            return (x - m) * jax.lax.rsqrt(v + eps) * g + b

        def _silu(x):
            return x * jax.nn.sigmoid(x)

        def _mamba(x, in_proj_w, conv_w, conv_b, x_proj_w, dt_proj_w, dt_proj_b, A_log, D_param, out_proj_w):
            xz = x @ in_proj_w.T
            xc, z = jnp.split(xz, 2, axis=-1)
            xc_t = xc.transpose(0, 2, 1)
            xc_t = jax.lax.conv_general_dilated(xc_t, conv_w, window_strides=(1,), padding=[(D_CONV - 1, 0)], dimension_numbers=('NCH', 'OIH', 'NCH'), feature_group_count=D_INNER) + conv_b[None, :, None]
            xc = _silu(xc_t).transpose(0, 2, 1)
            dbc = xc @ x_proj_w.T
            dt, Bm, Cm = jnp.split(dbc, [DT_RANK, DT_RANK + D_STATE], axis=-1)
            dt = jax.nn.softplus(dt @ dt_proj_w.T + dt_proj_b)
            A = -jnp.exp(A_log)

            def step(h, inp):
                dt_t, B_t, C_t, x_t = inp
                dA = jnp.exp(dt_t[..., None] * A)
                h = dA * h + (dt_t * x_t)[..., None] * B_t[:, None, :]
                y = jnp.einsum('bdn,bn->bd', h, C_t)
                return (h, y)
            h0 = jnp.zeros((x.shape[0], D_INNER, D_STATE), x.dtype)
            xs = (dt.transpose(1, 0, 2), Bm.transpose(1, 0, 2), Cm.transpose(1, 0, 2), xc.transpose(1, 0, 2))
            _, ys = jax.lax.scan(step, h0, xs)
            y = ys.transpose(1, 0, 2) + xc * D_param
            y = y * _silu(z)
            return y @ out_proj_w.T
        h = x + _mamba(_layernorm(x, norm1_g, norm1_b), in_proj_w, conv_w, conv_b, x_proj_w, dt_proj_w, dt_proj_b, A_log, D_param, out_proj_w)
        m = _layernorm(h, norm2_g, norm2_b)
        m = jax.nn.gelu(m @ mlp_w1.T + mlp_b1, approximate=False) @ mlp_w2.T + mlp_b2
        return h + m

    def _L0_ffn_ref(x, gate_w, wg, wu, wd, sg, su, sd):
        import jax, jax.numpy as jnp
        import numpy as np
        DIM = 256
        INTER = 128
        E = 8
        TOP_K = 2
        ROUTE_SCALE = 1.0
        B, S, D = x.shape
        xf = x.reshape(-1, D)
        N = xf.shape[0]
        scores = jax.nn.softmax(xf @ gate_w.T, axis=-1)
        _, idx = jax.lax.top_k(scores, TOP_K)
        weights = jnp.take_along_axis(scores, idx, axis=-1) * ROUTE_SCALE
        cw = jnp.zeros((N, E), dtype=xf.dtype)
        cw = cw.at[jnp.arange(N)[:, None], idx].add(weights)
        g = jnp.einsum('nd,efd->nef', xf, wg)
        u = jnp.einsum('nd,efd->nef', xf, wu)
        h = jax.nn.silu(g) * u
        y = jnp.einsum('nef,edf->ned', h, wd)
        routed = jnp.einsum('ned,ne->nd', y, cw)
        shared = jax.nn.silu(xf @ sg.T) * (xf @ su.T) @ sd.T
        return (routed + shared).reshape(B, S, D)
    x = L0_attn_x
    x = _layernorm(x + _L0_attn_ref(x, L0_attn_norm1_g, L0_attn_norm1_b, L0_attn_in_proj_w, L0_attn_conv_w, L0_attn_conv_b, L0_attn_x_proj_w, L0_attn_dt_proj_w, L0_attn_dt_proj_b, L0_attn_A_log, L0_attn_D_param, L0_attn_out_proj_w, L0_attn_norm2_g, L0_attn_norm2_b, L0_attn_mlp_w1, L0_attn_mlp_b1, L0_attn_mlp_w2, L0_attn_mlp_b2), axis=-1)
    x = _layernorm(x + _L0_ffn_ref(x, L0_ffn_gate_w, L0_ffn_wg, L0_ffn_wu, L0_ffn_wd, L0_ffn_sg, L0_ffn_su, L0_ffn_sd), axis=-1)
    return x

_drawn_inputs = setup_inputs


def setup_inputs(seed=0):
    import zlib

    import numpy as np

    out = dict(_drawn_inputs(seed))
    spreads = {'L0_attn_norm1_g': (1.0, 0.6),
     'L0_attn_norm1_b': (0.0, 0.8),
     'L0_attn_conv_b': (0.0, 0.8),
     'L0_attn_D_param': (1.0, 0.6),
     'L0_attn_norm2_g': (1.0, 0.6),
     'L0_attn_norm2_b': (0.0, 2.0),
     'L0_attn_mlp_b1': (0.0, 2.0),
     'L0_attn_mlp_b2': (0.0, 0.8)}
    factors = {'L0_attn_in_proj_w': 8.0,
     'L0_attn_conv_w': 8.0,
     'L0_attn_x_proj_w': 8.0,
     'L0_attn_dt_proj_w': 8.0,
     'L0_attn_dt_proj_b': 8.0,
     'L0_attn_A_log': 8.0,
     'L0_attn_out_proj_w': 8.0,
     'L0_attn_mlp_w1': 8.0,
     'L0_attn_mlp_w2': 8.0}
    for name, (base, spread) in spreads.items():
        noise = np.random.default_rng([zlib.crc32(name.encode()), seed]).standard_normal(out[name].shape)
        drawn = base * np.exp(spread * noise) if base else spread * noise
        out[name] = jnp.asarray(drawn.astype(out[name].dtype))
    for name, factor in factors.items():
        out[name] = (out[name] * factor).astype(out[name].dtype)
    return out
```

```python
import numpy as np
import concourse.bass as bass
from concourse import mybir
from contextlib import ExitStack


class Program:

    def __init__(self, nc, ctx):
        self.nc, self.ctx = nc, ctx
        self.queue = {e: [] for e in ("pe", "act", "dve", "pool", "sp")}
        self.sems, self.count, self.value, self.waited = {}, {}, {}, {}

    def sem(self, name):
        if name not in self.sems:
            self.sems[name] = self.ctx.enter_context(self.nc.semaphore("s_" + name))
            self.count[name] = 0
        return self.sems[name]

    def do(self, engine, instruction, step=None, at=None, by=1, lane=""):
        if step is None:
            self.queue[engine].append(instruction)
            return
        name = step + lane
        s = self.sem(name)
        self.count[name] += by
        self.value[step, at] = (name, self.count[name])
        self.queue[engine].append(lambda eng: instruction(eng).then_inc(s, by))

    def load(self, engine, instruction, step, at, lane=""):
        self.do(engine, instruction, step, at, by=16, lane=lane)

    def need(self, engine, step, at):
        name, v = self.value[step, at]
        if self.waited.get((engine, name), 0) < v:
            self.waited[engine, name] = v
            s = self.sems[name]
            self.queue[engine].append(lambda eng: eng.wait_ge(s, v))


def build(nc, a, out):
    F32 = mybir.dt.float32
    ALU = mybir.AluOpType
    ACT = mybir.ActivationFunctionType
    AX = mybir.AxisListType
    P = 128
    NB, T, D = a["x"].shape
    DI = a["conv_w"].shape[1] * P
    NS = a["A_log"].shape[2]
    NK = a["conv_w"].shape[2]
    NE = a["gate_w"].shape[2]
    NTB, KD, CT = T // P, D // P, DI // P
    R = a["dt_proj_w"].shape[0]
    NX = R + 2 * NS
    E0 = 64
    EPS = 1e-5
    HALF = T // 2
    CH = 4
    NCH = NS // CH

    ctx = ExitStack()
    with ctx:
        def sb(name, shape):
            return ctx.enter_context(nc.sbuf_tensor(name, shape, F32))

        p = Program(nc, ctx)
        do, need = p.do, p.need

        w_in = sb("w_in", [P, KD, 2 * DI])
        w_x = sb("w_x", [P, CT, NX])
        w_dt = sb("w_dt", [R, DI])
        w_out = sb("w_out", [P, CT, D])
        w_m1 = sb("w_m1", [P, KD, a["mlp_w1"].shape[2]])
        w_m2 = sb("w_m2", [P, CT, D])
        w_g = sb("w_g", [P, KD, (NE + 1) * P])
        w_u = sb("w_u", [P, KD, (NE + 1) * P])
        w_d = sb("w_d", [P, NE + 1, D])
        w_gate = sb("w_gate", [P, KD, NE])
        ident = sb("ident", [P, P])
        norm1 = sb("norm1", [P, 2, KD])
        norm2 = sb("norm2", [P, 2, KD])
        conv_w = sb("conv_w", [P, CT, NK])
        conv_b = sb("conv_b", [P, CT])
        dt_b = sb("dt_b", [P, CT])
        A = sb("A", [P, CT, NS])
        D_half = sb("D_half", [P, CT])
        b1 = sb("b1", [P, CT])
        b2 = sb("b2", [P, D])
        rank = sb("rank", [P, NTB, NE])
        m_half = sb("m_half", [P, NTB])

        xt = [sb(f"xt{i}", [P, NTB, D]) for i in range(3)]
        xnT = [sb(f"xnT{i}", [P, KD, T]) for i in range(2)]
        xc = [sb(f"xc{i}", [P, CT, T]) for i in range(2)]
        dt = [sb(f"dt{i}", [P, CT, T]) for i in range(2)]
        dtx = [sb(f"dtx{i}", [P, CT, T]) for i in range(2)]
        acc = [sb(f"acc{i}", [P, NTB, DI]) for i in range(2)]
        Bbc = [sb(f"Bbc{i}", [P, CH, T]) for i in range(2)]
        C_tok = [sb(f"C_tok{i}", [P, NTB, NS]) for i in range(2)]
        dBx = [sb(f"dBx{i}", [P, 2, T]) for i in range(3)]
        NHB = 2 * CT
        hs = [sb(f"hs{i}", [P, T]) for i in range(NHB)]
        pre_tmp = sb("pre_tmp", [P, CT, T])
        rows = sb("rows", [P, T])
        dbc, cwT = rows[0:NX, :], rows[E0:E0 + NE, :]
        h1 = sb("h1", [P, NTB, D])
        mT = sb("mT", [P, KD, T])
        post_tmp = sb("post_tmp", [P, CT, T])
        stats = {k: sb(f"stats_{k}", [P, NTB, 6]) for k in ("pre", "post")}
        mv = {k: sb(f"mv_{k}", [P, NTB, 2]) for k in ("pre", "post")}
        ve = {k: sb(f"ve_{k}", [P, NTB]) for k in ("pre", "post")}
        rs = {k: sb(f"rs_{k}", [P, NTB]) for k in ("pre", "post")}
        r1 = [sb(f"r1_{i}", [P, NTB]) for i in range(6)]
        r8 = [sb(f"r8_{i}", [P, NTB, NE]) for i in range(6)]

        NA, NH, ND = 2, 2, 4
        ps = [ctx.enter_context(nc.psum_tensor(f"ps{i}", [P, 512], F32)) for i in range(NA + NH + ND)]
        psA, psH, psD = ps[:NA], ps[NA:NA + NH], ps[NA + NH:]
        B_scratch = nc.dram_tensor("B_scratch", (NB, NS * T), F32, kind="Internal").ap()

        free_banks = [(i, None) for i in range(ND)]

        def take_bank():
            i, reader = free_banks.pop(0)
            if reader:
                need("pe", *reader)
            return i, psD[i]

        def give_bank(i, reader):
            free_banks.append((i, reader))

        nloads = [0]

        def bring(dst, src):
            p.load("sp", lambda e: e.dma_start(dst, src), "weights", nloads[0])
            nloads[0] += 1

        def constants():
            bring(norm1[:], a["norm1"])
            bring(w_in[:], a["in_proj_w"])
            for dst, key in ((conv_w, "conv_w"), (conv_b, "conv_b"), (w_x, "x_proj_w"), (w_dt, "dt_proj_w"),
                             (dt_b, "dt_proj_b"), (A, "A_log"), (D_half, "D_param"), (w_out, "out_proj_w"),
                             (norm2, "norm2"), (w_m1, "mlp_w1"), (b1, "mlp_b1"), (w_m2, "mlp_w2"),
                             (w_gate, "gate_w"), (w_g, "wg"), (w_u, "wu"), (w_d, "wd")):
                bring(dst[:], a[key])
            bring(b2[:], a["mlp_b2"].broadcast_to([P, D]))
            last = nloads[0] - 1
            do("pool", lambda e: e.memset(ident[:], 0.0), "zeroed", 0)
            do("pool", lambda e: e.memset(m_half[:], -0.5), "consts", 0)
            for k in range(NE):
                do("pool", lambda e, k=k: e.memset(rank[:, :, k:k + 1], float(NE - k)), "consts", 1 + k)
            need("pool", "zeroed", 0)
            do("pool", lambda e: e.affine_select(out=ident[:], in_=ident[:], compare_op=ALU.not_equal, fill=1.0,
                                                 base=0, pattern=[[-1, P]], channel_multiplier=1),
               "consts", "all")
            need("dve", "weights", last)
            halves = [(w_x[:], 0.5), (w_x[:, :, R:R + NS], 0.5), (w_out[:], 0.5), (w_d[:], 0.5), (D_half[:], 0.5)]
            for k, (w, f) in enumerate(halves):
                if k == 1:
                    need("dve", "halved", 0)
                do("dve", lambda e, w=w, f=f: e.tensor_scalar(w, w, f, None, ALU.mult), "halved", k)
            need("act", "weights", last)
            do("act", lambda e: e.activation(A[:], A[:], ACT.Exp), "A_exp", 0)
            need("dve", "A_exp", 0)
            do("dve", lambda e: e.tensor_scalar(A[:], A[:], -1.0, None, ALU.mult), "halved", "all")
            for e in ("act", "pe", "pool", "dve"):
                need(e, "weights", last)
                need(e, "halved", "all")
                need(e, "consts", "all")

        def ln_stats(k, src, b):
            for i in range(NTB):
                do("dve", lambda e, i=i: e.bn_stats(stats[k][:, i, :], src[:, i, :]), "bn_" + k, (b, i))
            need("dve", "bn_" + k, (b, NTB - 1))
            if ("rstd_" + k, prev_ln[k]) in p.value:
                need("dve", "rstd_" + k, prev_ln[k])
            for i in range(NTB):
                do("dve", lambda e, i=i: e.bn_aggr(mv[k][:, i, :], stats[k][:, i, :]), "mean_" + k, (b, i))
            need("dve", "mean_" + k, (b, NTB - 1))
            do("dve", lambda e: e.tensor_scalar(ve[k][:], mv[k][:, :, 1], EPS, None, ALU.add), "var_" + k, b)
            need("pool", "var_" + k, b)
            if ("norm_" + k, prev_ln[k]) in p.value:
                need("pool", "norm_" + k, prev_ln[k])
            do("pool", lambda e: e.tensor_tensor(rs[k][:], ve[k][:], m_half[:], ALU.pow), "rstd_" + k, b)
            prev_ln[k] = b

        prev_ln = {"pre": None, "post": None}

        def ln_apply(k, src, dst, b):
            need("dve", "rstd_" + k, b)
            for i in range(NTB):
                do("dve", lambda e, i=i: e.tensor_scalar(dst[:, i, :], src[:, i, :], mv[k][:, i, 0:1],
                                                         rs[k][:, i:i + 1], ALU.subtract, ALU.mult), "norm_" + k,
                   b if i == NTB - 1 else (b, i))

        def to_channels(src, ready, evict):
            for kt in range(KD):
                i, bank = take_bank()
                need("pe", *ready)
                for t in range(NTB):
                    fn = lambda e, t=t, kt=kt, bank=bank: e.transpose(
                        bank[:, t * P:(t + 1) * P], src[:, t, kt * P:(kt + 1) * P], ident[:])
                    if t == NTB - 1:
                        do("pe", fn, "turned", p.count.get("turned", 0))
                    else:
                        do("pe", fn)
                need("act", "turned", p.count["turned"] - 1)
                evict(kt, bank, i)

        def scaled_evict(norm, dst, step, b):
            def evict(kt, bank, i):
                do("act", lambda e: e.activation(dst[:, kt, :], bank[:], ACT.Identity, scale=norm[:, 0, kt:kt + 1],
                                                 bias=norm[:, 1, kt:kt + 1]), step, (b, kt))
                give_bank(i, (step, (b, kt)))
            return evict

        def pre(b):
            x, xn, c, s2 = xt[b % 3], xnT[b % 2], xc[b % 2], b % 2
            if b >= 3:
                need("sp", "stored", b - 3)
            p.load("sp", lambda e: e.dma_start(x[:], a["x"][b].rearrange("(t p) d -> p t d", p=P)),
                   "x_in", b, lane=str(b % 3))
            yield
            need("dve", "x_in", b)
            ln_stats("pre", x, b)
            yield
            yield
            tok = pre_tmp[:, 0:2, :].rearrange("p a (t d) -> p (a t) d", d=D)
            if b:
                need("dve", "dt_sum", b - 1)
            ln_apply("pre", x, tok, b)
            yield
            if b >= 2:
                need("act", "z_mm", (b - 2, CT - 1))
            to_channels(tok, ("norm_pre", b), scaled_evict(norm1, xn, "xnT", b))
            yield
            for j in range(CT):
                i, bank = take_bank()
                need("pe", "xnT", (b, KD - 1))
                for k in range(KD):
                    fn = lambda e, j=j, k=k, bank=bank: e.matmul(
                        bank[:], w_in[:, k, j * P:(j + 1) * P], xn[:, k, :], start=(k == 0), stop=(k == KD - 1))
                    do("pe", fn, *(("in_mm", (b, j)) if k == KD - 1 else ()))
                need("act", "in_mm", (b, j))
                if b >= 2:
                    need("act", "out_mm", (b - 2, 1))
                do("act", lambda e, j=j, bank=bank: e.activation(
                    c[:, j, :], bank[:], ACT.Identity, scale=conv_w[:, j, NK - 1:NK], bias=conv_b[:, j:j + 1]),
                    "tap0", (b, j))
                yield
                need("dve", "tap0", (b, j))
                for s in range(1, NK):
                    if s > 1:
                        need("dve", "tap", (b, j, s - 1))
                    do("dve", lambda e, j=j, s=s, bank=bank: e.scalar_tensor_tensor(
                        out=c[:, j, s:], in0=bank[:, 0:T - s], scalar=conv_w[:, j, NK - 1 - s:NK - s],
                        in1=c[:, j, s:], op0=ALU.mult, op1=ALU.add), "tap", (b, j, s))
                give_bank(i, ("tap", (b, j, NK - 1)))
                need("act", "tap", (b, j, NK - 1))
                do("act", lambda e, j=j: e.activation(pre_tmp[:, j, :], c[:, j, :], ACT.Tanh, scale=0.5),
                   "tanh_x", (b, j))
                yield
                need("dve", "tanh_x", (b, j))
                do("dve", lambda e, j=j: e.scalar_tensor_tensor(
                    out=c[:, j, :], in0=pre_tmp[:, j, :], scalar=1.0, in1=c[:, j, :], op0=ALU.add, op1=ALU.mult),
                    "silu_x", (b, j))
            yield
            i, bank = take_bank()
            need("pe", "silu_x", (b, CT - 1))
            for k in range(CT):
                fn = lambda e, k=k, bank=bank: e.matmul(bank[0:NX, :], w_x[:, k, :], c[:, k, :], start=(k == 0),
                                                        stop=(k == CT - 1))
                do("pe", fn, *(("x_mm", b) if k == CT - 1 else ()))
            need("act", "x_mm", b)
            if b:
                need("act", "B_out", b - 1)
            do("act", lambda e, bank=bank: e.activation(dbc, bank[0:NX, :], ACT.Copy), "dbc", b)
            give_bank(i, ("dbc", b))
            need("sp", "dbc", b)
            p.load("sp", lambda e: e.dma_start(B_scratch[b].rearrange("(n t) -> n t", t=T), dbc[R:R + NS, :]),
                   "B_out", b)
            yield
            i, bank = take_bank()
            need("pe", "dbc", b)
            for t in range(NTB):
                fn = lambda e, t=t, bank=bank: e.transpose(bank[:, t * NS:(t + 1) * NS],
                                                           dbc[R + NS:NX, t * P:(t + 1) * P],
                                                           ident[R + NS:NX, R + NS:NX])
                do("pe", fn, *(("C_turned", b) if t == NTB - 1 else ()))
            need("act", "C_turned", b)
            if b >= 2:
                need("act", "weighed", ((b - 2) * NS + NS - 1) * NTB + NTB - 1)
            do("act", lambda e, bank=bank: e.activation(C_tok[s2][:], bank[:, 0:NTB * NS].rearrange(
                "p (t n) -> p t n", n=NS), ACT.Copy), "C_tok", b)
            give_bank(i, ("C_tok", b))
            for j in range(CT):
                i, bank = take_bank()
                do("pe", lambda e, j=j, bank=bank: e.matmul(bank[:], w_dt[:, j * P:(j + 1) * P], dbc[0:R, :],
                                                            start=True, stop=True), "dt_mm", (b, j))
                need("act", "dt_mm", (b, j))
                need("act", "silu_x", (b, j))
                do("act", lambda e, j=j, bank=bank: e.activation(pre_tmp[:, j, :], bank[:], ACT.Abs,
                                                                 bias=dt_b[:, j:j + 1]), "dt_abs", (b, j))
                need("dve", "dt_abs", (b, j))
                if b >= 2:
                    need("dve", "dA", ((b - 2) * NS + NS - 1) * CT + CT - 1)
                do("dve", lambda e, j=j, bank=bank: e.tensor_scalar(dt[s2][:, j, :], bank[:], dt_b[:, j:j + 1], 0.0,
                                                                    ALU.add, ALU.max), "dt_relu", (b, j))
                give_bank(i, ("dt_relu", (b, j)))
                yield
            need("act", "dt_abs", (b, CT - 1))
            do("act", lambda e: e.activation(pre_tmp[:], pre_tmp[:], ACT.Exp, scale=-1.0), "dt_exp", b)
            need("act", "dt_exp", b)
            do("act", lambda e: e.activation(pre_tmp[:], pre_tmp[:], ACT.Ln, bias=1.0), "dt_ln", b)
            yield
            need("pool", "dt_ln", b)
            need("pool", "dt_relu", (b, CT - 1))
            do("pool", lambda e: e.tensor_tensor(dt[s2][:], dt[s2][:], pre_tmp[:], ALU.add), "dt_sum", b)
            need("pool", "dt_sum", b)
            need("pool", "silu_x", (b, CT - 1))
            do("pool", lambda e: e.tensor_tensor(dtx[s2][:], dt[s2][:], c[:], ALU.mult), "dtx", b)

        def load_B(b, ch):
            g = b * NCH + ch
            if g >= 2:
                need("sp", "dBx", ((g - 2) * CH + CH - 1) * 2 + 1)
            need("sp", "B_out", b)
            p.load("sp", lambda e: e.dma_start(
                Bbc[g % 2][:].rearrange("p n t -> p (n t)"),
                B_scratch[b:b + 1, ch * CH * T:(ch + 1) * CH * T].broadcast_to([P, CH * T])),
                "B_in", g, lane=str(g % 2))

        def make_dBx(b, n, q):
            g = b * NCH + n // CH
            need("pool", "B_in", g)
            need("pool", "dtx", b)
            u = (b * NS + n) * 2 + q
            if u >= 3:
                need("pool", "scan", (u - 3) * 2 + 1)
            do("pool", lambda e: e.tensor_tensor(
                dBx[u % 3][:], dtx[b % 2][:, 2 * q:2 * q + 2, :],
                Bbc[g % 2][:, n % CH:n % CH + 1, :].broadcast_to([P, 2, T]), ALU.mult), "dBx", u)

        def scan(b, n, j):
            s = (b * NS + n) * CT + j
            if s >= NA:
                need("act", "scan", s - NA)
            need("act", "dt_sum", b)
            do("act", lambda e: e.activation(psA[s % NA][:], dt[b % 2][:, j, :], ACT.Exp, scale=A[:, j, n:n + 1]),
               "dA", s)
            need("dve", "dA", s)
            need("dve", "dBx", s // 2)
            if s >= NHB:
                need("dve", "h_turned", (s - NHB) // CT * NTB + NTB - 1)
            do("dve", lambda e: e.tensor_tensor_scan(hs[s % NHB][:], psA[s % NA][:], dBx[s // 2 % 3][:, s % 2, :],
                                                     0.0, ALU.mult, ALU.add), "scan", s)

        def weigh(b, n, t):
            w = (b * NS + n) * NTB + t
            if w >= NH:
                need("pe", "weighed", w - NH)
            need("pe", "scan", (b * NS + n) * CT + CT - 1)
            for j in range(CT):
                s = (b * NS + n) * CT + j
                fn = lambda e, j=j, s=s: e.transpose(psH[w % NH][:, j * P:(j + 1) * P],
                                                     hs[s % NHB][:, t * P:(t + 1) * P], ident[:])
                do("pe", fn, *(("h_turned", w) if j == CT - 1 else ()))
            need("dve", "h_turned", w)
            need("dve", "C_tok", b)
            o = acc[b % 2][:, t, :]
            if n == 0:
                if b >= 2:
                    need("dve", "y_turned", (b - 2, CT - 1))
                do("dve", lambda e: e.tensor_scalar(o, psH[w % NH][:], C_tok[b % 2][:, t, n:n + 1], None, ALU.mult),
                   "weighed", w)
            else:
                need("dve", "weighed", w - NTB)
                do("dve", lambda e: e.scalar_tensor_tensor(out=o, in0=psH[w % NH][:],
                                                           scalar=C_tok[b % 2][:, t, n:n + 1], in1=o,
                                                           op0=ALU.mult, op1=ALU.add), "weighed", w)

        def post(b):
            x, xn, c = xt[b % 3], xnT[b % 2], xc[b % 2]
            zt = post_tmp
            for j in range(CT):
                i, bank = take_bank()
                for k in range(KD):
                    fn = lambda e, j=j, k=k, bank=bank: e.matmul(
                        bank[:], w_in[:, k, DI + j * P:DI + (j + 1) * P], xn[:, k, :], start=(k == 0),
                        stop=(k == KD - 1))
                    do("pe", fn, *(("z_mm", (b, j)) if k == KD - 1 else ()))
                need("act", "z_mm", (b, j))
                if b:
                    need("act", "down_mm", (b - 1, 1, NE))
                do("act", lambda e, j=j, bank=bank: e.activation(zt[:, j, :], bank[:], ACT.Tanh, scale=0.5),
                   "tanh_z", (b, j))
                yield
                need("dve", "tanh_z", (b, j))
                do("dve", lambda e, j=j, bank=bank: e.scalar_tensor_tensor(
                    out=zt[:, j, :], in0=zt[:, j, :], scalar=1.0, in1=bank[:], op0=ALU.add, op1=ALU.mult),
                    "silu_z", (b, j))
                give_bank(i, ("silu_z", (b, j)))
                i, bank = take_bank()
                need("pe", "weighed", (b * NS + NS - 1) * NTB + NTB - 1)
                for t in range(NTB):
                    fn = lambda e, j=j, t=t, bank=bank: e.transpose(
                        bank[:, t * P:(t + 1) * P], acc[b % 2][:, t, j * P:(j + 1) * P], ident[:])
                    do("pe", fn, *(("y_turned", (b, j)) if t == NTB - 1 else ()))
                need("dve", "y_turned", (b, j))
                do("dve", lambda e, j=j, bank=bank: e.scalar_tensor_tensor(
                    out=c[:, j, :], in0=c[:, j, :], scalar=D_half[:, j:j + 1], in1=bank[:], op0=ALU.mult,
                    op1=ALU.add), "y_plus", (b, j))
                give_bank(i, ("y_plus", (b, j)))
                need("pool", "y_plus", (b, j))
                do("pool", lambda e, j=j: e.tensor_tensor(c[:, j, :], c[:, j, :], zt[:, j, :], ALU.mult),
                   "gated", (b, j))
            yield
            for q in range(2):
                i, bank = take_bank()
                need("pe", "gated", (b, CT - 1))
                for t in range(2):
                    for k in range(CT):
                        fn = lambda e, q=q, t=t, k=k, bank=bank: e.matmul(
                            bank[:, t * D:(t + 1) * D], c[:, k, (2 * q + t) * P:(2 * q + t + 1) * P], w_out[:, k, :],
                            start=(k == 0), stop=(k == CT - 1))
                        do("pe", fn, *(("out_mm", (b, q)) if (t, k) == (1, CT - 1) else ()))
                need("dve", "out_mm", (b, q))
                do("dve", lambda e, q=q, bank=bank: e.tensor_tensor(
                    h1[:, 2 * q:2 * q + 2, :], bank[:].rearrange("p (t d) -> p t d", d=D), x[:, 2 * q:2 * q + 2, :],
                    ALU.add), "h1", (b, q))
                give_bank(i, ("h1", (b, q)))
                yield
            need("pool", "h1", (b, 1))
            do("pool", lambda e: e.tensor_tensor(x[:], x[:], h1[:], ALU.add), "x_plus", b)
            need("pool", "x_plus", b)
            do("pool", lambda e: e.tensor_tensor(x[:], x[:], b2[:].rearrange("p (a d) -> p a d", a=1).broadcast_to(
                [P, NTB, D]), ALU.add), "x_plus2", b)
            need("dve", "h1", (b, 1))
            ln_stats("post", h1, (b, 2))
            yield
            tok = post_tmp[:, 0:2, :].rearrange("p a (t d) -> p (a t) d", d=D)
            need("dve", "gated", (b, CT - 1))
            ln_apply("post", h1, tok, (b, 2))
            yield
            to_channels(tok, ("norm_post", (b, 2)), scaled_evict(norm2, mT, "mT", b))
            yield
            for j in range(CT):
                i, bank = take_bank()
                need("pe", "mT", (b, KD - 1))
                for k in range(KD):
                    fn = lambda e, j=j, k=k, bank=bank: e.matmul(
                        bank[:], w_m1[:, k, j * P:(j + 1) * P], mT[:, k, :], start=(k == 0), stop=(k == KD - 1))
                    do("pe", fn, *(("m1_mm", (b, j)) if k == KD - 1 else ()))
                need("act", "m1_mm", (b, j))
                do("act", lambda e, j=j, bank=bank: e.activation(post_tmp[:, j, :], bank[:], ACT.Gelu,
                                                                 bias=b1[:, j:j + 1]), "gelu", (b, j))
                give_bank(i, ("gelu", (b, j)))
                if j % 2:
                    yield
            for q in range(2):
                i, bank = take_bank()
                need("pe", "gelu", (b, CT - 1))
                for t in range(2):
                    for k in range(CT):
                        fn = lambda e, q=q, t=t, k=k, bank=bank: e.matmul(
                            bank[:, t * D:(t + 1) * D], post_tmp[:, k, (2 * q + t) * P:(2 * q + t + 1) * P],
                            w_m2[:, k, :], start=(k == 0), stop=(k == CT - 1))
                        do("pe", fn, *(("m2_mm", (b, q)) if (t, k) == (1, CT - 1) else ()))
                need("dve", "m2_mm", (b, q))
                need("dve", "x_plus2", b)
                do("dve", lambda e, q=q, bank=bank: e.tensor_tensor(
                    x[:, 2 * q:2 * q + 2, :], bank[:].rearrange("p (t d) -> p t d", d=D), x[:, 2 * q:2 * q + 2, :],
                    ALU.add), "r", (b, q))
                give_bank(i, ("r", (b, q)))
                yield
            need("dve", "r", (b, 1))
            ln_stats("post", x, (b, 3))
            yield
            ln_apply("post", x, h1, (b, 3))
            yield

            def plain_evict(kt, bank, i):
                do("act", lambda e: e.activation(mT[:, kt, :], bank[:], ACT.Copy), "x2T", (b, kt))
                give_bank(i, ("x2T", (b, kt)))
            to_channels(h1, ("norm_post", (b, 3)), plain_evict)
            yield
            i, bank = take_bank()
            need("pe", "x2T", (b, KD - 1))
            for t in range(NTB):
                for k in range(KD):
                    fn = lambda e, t=t, k=k, bank=bank: e.matmul(bank[:, t * NE:(t + 1) * NE],
                                                                 mT[:, k, t * P:(t + 1) * P], w_gate[:, k, :],
                                                                 start=(k == 0), stop=(k == KD - 1))
                    do("pe", fn, *(("gate_mm", b) if (t, k) == (NTB - 1, KD - 1) else ()))
            need("dve", "gate_mm", b)
            lg = bank[:, 0:NTB * NE].rearrange("p (t e) -> p t e", e=NE)
            mx, sm, top1, key1, top2, key2 = r1
            pr, eq, key, one1, rest, cw = r8

            def wide(v):
                return v[:].rearrange("p (t o) -> p t o", o=1).broadcast_to([P, NTB, NE])

            nr = [0]

            def route(fn):
                if nr[0]:
                    need("dve", "route", (b, nr[0] - 1))
                do("dve", fn, "route", (b, nr[0]))
                nr[0] += 1

            route(lambda e: e.tensor_reduce(mx[:], lg, AX.X, ALU.max))
            route(lambda e: e.tensor_tensor(pr[:], lg, wide(mx), ALU.subtract))
            give_bank(i, ("route", (b, nr[0] - 1)))
            need("act", "route", (b, nr[0] - 1))
            do("act", lambda e: e.activation(pr[:], pr[:], ACT.Exp), "route_exp", b)
            yield
            need("dve", "route_exp", b)
            route(lambda e: e.tensor_reduce(sm[:], pr[:], AX.X, ALU.add))
            route(lambda e: e.reciprocal(sm[:], sm[:]))
            route(lambda e: e.tensor_tensor(pr[:], pr[:], wide(sm), ALU.mult))
            route(lambda e: e.tensor_reduce(top1[:], pr[:], AX.X, ALU.max))
            route(lambda e: e.tensor_tensor(eq[:], pr[:], wide(top1), ALU.is_equal))
            route(lambda e: e.tensor_tensor(key[:], eq[:], rank[:], ALU.mult))
            route(lambda e: e.tensor_reduce(key1[:], key[:], AX.X, ALU.max))
            route(lambda e: e.tensor_tensor(one1[:], rank[:], wide(key1), ALU.is_equal))
            route(lambda e: e.scalar_tensor_tensor(out=rest[:], in0=one1[:], scalar=-2.0, in1=pr[:], op0=ALU.mult,
                                                   op1=ALU.add))
            yield
            route(lambda e: e.tensor_reduce(top2[:], rest[:], AX.X, ALU.max))
            route(lambda e: e.tensor_tensor(eq[:], rest[:], wide(top2), ALU.is_equal))
            route(lambda e: e.tensor_tensor(key[:], eq[:], rank[:], ALU.mult))
            route(lambda e: e.tensor_reduce(key2[:], key[:], AX.X, ALU.max))
            route(lambda e: e.tensor_tensor(eq[:], rank[:], wide(key2), ALU.is_equal))
            route(lambda e: e.tensor_tensor(eq[:], eq[:], one1[:], ALU.add))
            route(lambda e: e.tensor_tensor(cw[:], eq[:], pr[:], ALU.mult))
            i, bank = take_bank()
            need("pe", "route", (b, nr[0] - 1))
            for t in range(NTB):
                fn = lambda e, t=t, bank=bank: e.transpose(bank[0:NE, t * P:(t + 1) * P], cw[:, t, :], ident[:])
                do("pe", fn, *(("cw_turned", b) if t == NTB - 1 else ()))
            need("act", "cw_turned", b)
            do("act", lambda e, bank=bank: e.activation(cwT, bank[0:NE, :], ACT.Copy), "cwT", b)
            give_bank(i, ("cwT", b))
            yield
            NG = 4
            gt = [post_tmp[:, 2 + k // 2, (k % 2) * HALF:(k % 2 + 1) * HALF] for k in range(NG)]
            def experts(q):
                yi, ybank = take_bank()
                ts = slice(q * HALF, (q + 1) * HALF)

                def up(x_):
                    v = q * (NE + 1) + x_
                    g = gt[v % NG]
                    i, bank = take_bank()
                    for o, w in ((0, w_g), (HALF, w_u)):
                        for k in range(KD):
                            fn = lambda e, o=o, w=w, k=k, bank=bank: e.matmul(
                                bank[:, o:o + HALF], w[:, k, x_ * P:(x_ + 1) * P], mT[:, k, ts], start=(k == 0),
                                stop=(k == KD - 1))
                            do("pe", fn, *(("gu_mm", (b, v)) if (o, k) == (HALF, KD - 1) else ()))
                    need("act", "gu_mm", (b, v))
                    if v >= NG:
                        need("act", "down_mm", (b, (v - NG) // (NE + 1), (v - NG) % (NE + 1)))
                    do("act", lambda e, bank=bank: e.activation(g, bank[:, 0:HALF], ACT.Tanh, scale=0.5),
                       "tanh_g", (b, v))
                    return i, bank, g, v

                def weigh_expert(x_, i, bank, g, v):
                    if x_ < NE:
                        ci, cbank = take_bank()
                        need("pe", "cwT", b)
                        do("pe", lambda e, cbank=cbank: e.matmul(cbank[:, 0:HALF], ident[E0:E0 + NE, E0 + x_:E0 + x_ + 1].broadcast_to([NE, P]), cwT[:, ts],
                                                                 start=True, stop=True), "cw_mm", (b, v))
                    need("dve", "tanh_g", (b, v))
                    do("dve", lambda e, bank=bank: e.scalar_tensor_tensor(
                        out=g, in0=g, scalar=1.0, in1=bank[:, 0:HALF], op0=ALU.add, op1=ALU.mult), "silu_g", (b, v))
                    need("dve", "silu_g", (b, v))
                    do("dve", lambda e, bank=bank: e.tensor_tensor(g, g, bank[:, HALF:T], ALU.mult), "hidden", (b, v))
                    give_bank(i, ("hidden", (b, v)))
                    if x_ < NE:
                        need("dve", "hidden", (b, v))
                        need("dve", "cw_mm", (b, v))
                        do("dve", lambda e, cbank=cbank: e.tensor_tensor(g, g, cbank[:, 0:HALF], ALU.mult),
                           "weighted", (b, v))
                        give_bank(ci, ("weighted", (b, v)))

                def down(x_, g, v):
                    need("pe", "weighted" if x_ < NE else "hidden", (b, v))
                    for t in range(2):
                        fn = lambda e, t=t: e.matmul(ybank[:, t * D:(t + 1) * D], g[:, t * P:(t + 1) * P],
                                                     w_d[:, x_, :], start=(x_ == 0 and t == 0),
                                                     stop=(x_ == NE), skip_group_check=True)
                        do("pe", fn, *(("down_mm", (b, q, x_)) if t else ()))

                late = None
                for x_ in range(NE + 1):
                    made = up(x_)
                    yield
                    weigh_expert(x_, *made)
                    if late:
                        down(*late)
                    late = (x_, made[2], made[3])
                yield
                down(*late)
                need("dve", "down_mm", (b, q, NE))
                need("dve", "norm_post", (b, 3))
                do("dve", lambda e, q=q: e.tensor_tensor(
                    x[:, 2 * q:2 * q + 2, :], ybank[:].rearrange("p (t d) -> p t d", d=D),
                    h1[:, 2 * q:2 * q + 2, :], ALU.add), "r2", (b, q))
                give_bank(yi, ("r2", (b, q)))
                yield
            for q in range(2):
                yield from experts(q)
            need("dve", "r2", (b, 1))
            ln_stats("post", x, (b, 4))
            yield
            ln_apply("post", x, x, (b, 4))
            need("sp", "norm_post", (b, 4))
            p.load("sp", lambda e: e.dma_start(out[b].rearrange("(t p) d -> p t d", p=P), x[:]), "stored", b,
                   lane=str(b % 3))

        def run(gen, steps=10 ** 9):
            for _ in range(steps):
                if next(gen, run) is run:
                    return

        constants()
        run(pre(0))
        load_B(0, 0)
        load_B(0, 1)
        make_dBx(0, 0, 0)
        make_dBx(0, 0, 1)
        for b in range(NB + 1):
            behind = post(b - 1) if b else iter(())
            ahead = pre(b + 1) if b + 1 < NB else iter(())
            for n in range(NS):
                if b < NB:
                    for j in range(CT):
                        if n + 1 < NS and j % 2 == 0:
                            make_dBx(b, n + 1, j // 2)
                        scan(b, n, j)
                        if n:
                            weigh(b, n - 1, j)
                        elif b:
                            weigh(b - 1, NS - 1, j)
                        if n or j == CT - 1:
                            run(behind, 1)
                        if n >= 5 and j % 2:
                            run(ahead, 1)
                    if n % CH == CH - 1:
                        ch = n // CH + 2
                        if ch < NCH:
                            load_B(b, ch)
                else:
                    if n == 0:
                        for j in range(NTB):
                            weigh(b - 1, NS - 1, j)
                    run(behind, 4)
            run(behind)
            run(ahead)
            if b + 1 < NB:
                load_B(b + 1, 0)
                load_B(b + 1, 1)
                make_dBx(b + 1, 0, 0)
                make_dBx(b + 1, 0, 1)
        for b in range(max(0, NB - 3), NB):
            need("sp", "stored", b)

        block = ctx.enter_context(nc.Block())

        @block.sync
        def _(eng):
            for f in p.queue["sp"]:
                f(eng)

        @block.gpsimd
        def _(eng):
            for f in p.queue["pool"]:
                f(eng)

        @block.scalar
        def _(eng):
            for f in p.queue["act"]:
                f(eng)

        @block.tensor
        def _(eng):
            for f in p.queue["pe"]:
                f(eng)

        @block.vector
        def _(eng):
            for f in p.queue["dve"]:
                f(eng)


def lay_out(i):
    def tiles(w):
        k, m = w.shape
        return w.reshape(k // 128, 128, m).transpose(1, 0, 2)

    def cols(v):
        return v.reshape(-1, 128).T

    g = {k: np.asarray(v) for k, v in i.items()}
    L = lambda k: g["L0_attn_" + k]
    E = lambda k: g["L0_ffn_" + k]
    wg = np.concatenate([E("wg"), E("sg")[None]]).reshape(-1, 256)
    wu = np.concatenate([E("wu"), E("su")[None]]).reshape(-1, 256)
    wd = np.concatenate([E("wd"), E("sd")[None]])
    return {
        "x": L("x"), "norm1": np.stack([cols(L("norm1_g")), cols(L("norm1_b"))], 1),
        "norm2": np.stack([cols(L("norm2_g")), cols(L("norm2_b"))], 1),
        "in_proj_w": tiles(L("in_proj_w").T), "conv_w": tiles(L("conv_w")[:, 0, :]), "conv_b": cols(L("conv_b")),
        "x_proj_w": tiles(L("x_proj_w").T), "dt_proj_w": L("dt_proj_w").T, "dt_proj_b": cols(L("dt_proj_b")),
        "A_log": tiles(L("A_log")), "D_param": cols(L("D_param")), "out_proj_w": tiles(L("out_proj_w").T),
        "mlp_w1": tiles(L("mlp_w1").T), "mlp_b1": cols(L("mlp_b1")), "mlp_w2": tiles(L("mlp_w2").T),
        "mlp_b2": L("mlp_b2")[None, :], "gate_w": tiles(E("gate_w").T), "wg": tiles(wg.T), "wu": tiles(wu.T),
        "wd": wd.transpose(2, 0, 1),
    }


def kernel(**inputs):
    import concourse.bacc as bacc
    from concourse.bass_utils import run_bass_kernel_spmd

    nc = bacc.Bacc("TRN2", target_bir_lowering=False, num_devices=1)
    arrays, aps = {}, {}
    for name, v in lay_out(inputs).items():
        v = np.ascontiguousarray(v)
        arrays[f"in_{name}"] = v
        aps[name] = nc.dram_tensor(f"in_{name}", v.shape, mybir.dt.from_np(v.dtype), kind="ExternalInput").ap()
    out = nc.dram_tensor("out", aps["x"].shape, mybir.dt.float32, kind="ExternalOutput").ap()
    build(nc, aps, out)
    return run_bass_kernel_spmd(nc, [arrays], core_ids=[0]).results[0]["out"]
```

```python
import numpy as np
import concourse.bass as bass
from concourse import mybir
from contextlib import ExitStack


class Program:

    def __init__(self, nc, ctx):
        self.nc, self.ctx = nc, ctx
        self.queue = {e: [] for e in ("pe", "act", "dve", "pool", "sp")}
        self.sems, self.count, self.value, self.waited = {}, {}, {}, {}

    def sem(self, name):
        if name not in self.sems:
            self.sems[name] = self.ctx.enter_context(self.nc.semaphore("s_" + name))
            self.count[name] = 0
        return self.sems[name]

    def do(self, engine, instruction, step=None, at=None, by=1, lane=""):
        if step is None:
            self.queue[engine].append(instruction)
            return
        name = step + lane
        s = self.sem(name)
        self.count[name] += by
        self.value[step, at] = (name, self.count[name])
        self.queue[engine].append(lambda eng: instruction(eng).then_inc(s, by))

    def load(self, engine, instruction, step, at, lane=""):
        self.do(engine, instruction, step, at, by=16, lane=lane)

    def need(self, engine, step, at):
        name, v = self.value[step, at]
        if self.waited.get((engine, name), 0) < v:
            self.waited[engine, name] = v
            s = self.sems[name]
            self.queue[engine].append(lambda eng: eng.wait_ge(s, v))


def build(nc, a, out):
    F32 = mybir.dt.float32
    ALU = mybir.AluOpType
    ACT = mybir.ActivationFunctionType
    AX = mybir.AxisListType
    P = 128
    NB, T, D = a["x"].shape
    DI = a["conv_w"].shape[1] * P
    NS = a["A_log"].shape[2]
    NK = a["conv_w"].shape[2]
    NE = a["gate_w"].shape[2]
    NTB, KD, CT = T // P, D // P, DI // P
    R = a["dt_proj_w"].shape[0]
    NX = R + 2 * NS
    E0 = 64
    EPS = 1e-5
    HALF = T // 2
    CH, NBB = 2, 3
    NCH = NS // CH

    ctx = ExitStack()
    with ctx:
        def sb(name, shape):
            return ctx.enter_context(nc.sbuf_tensor(name, shape, F32))

        p = Program(nc, ctx)
        do, need = p.do, p.need

        w_in = sb("w_in", [P, KD, 2 * DI])
        w_x = sb("w_x", [P, CT, NX])
        w_dt = sb("w_dt", [R, DI])
        w_out = sb("w_out", [P, CT, D])
        w_m1 = sb("w_m1", [P, KD, a["mlp_w1"].shape[2]])
        w_m2 = sb("w_m2", [P, CT, D])
        w_g = sb("w_g", [P, KD, (NE + 1) * P])
        w_u = sb("w_u", [P, KD, (NE + 1) * P])
        w_d = sb("w_d", [P, NE + 1, D])
        w_gate = sb("w_gate", [P, KD, NE])
        ident = sb("ident", [P, P])
        norm1 = sb("norm1", [P, 2, KD])
        norm2 = sb("norm2", [P, 2, KD])
        conv_w = sb("conv_w", [P, CT, NK])
        conv_b = sb("conv_b", [P, CT])
        dt_b = sb("dt_b", [P, CT])
        A = sb("A", [P, CT, NS])
        D_half = sb("D_half", [P, CT])
        b1 = sb("b1", [P, CT])
        b2 = sb("b2", [P, D])
        rank = sb("rank", [P, NTB, NE])
        m_half = sb("m_half", [P, NTB])

        xt = [sb(f"xt{i}", [P, NTB, D]) for i in range(3)]
        xnT = [sb(f"xnT{i}", [P, KD, T]) for i in range(2)]
        xc = [sb(f"xc{i}", [P, CT, T]) for i in range(2)]
        dt = [sb(f"dt{i}", [P, CT, T]) for i in range(2)]
        dtx = [sb(f"dtx{i}", [P, CT, T]) for i in range(2)]
        acc = [sb(f"acc{i}", [P, NTB, DI]) for i in range(2)]
        Bbc = [sb(f"Bbc{i}", [P, CH, T]) for i in range(NBB)]
        C_tok = [sb(f"C_tok{i}", [P, NTB, NS]) for i in range(2)]
        dBx = [sb(f"dBx{i}", [P, 2, T]) for i in range(3)]
        NHB = 3 * CT
        hs = [sb(f"hs{i}", [P, T]) for i in range(NHB)]
        pre_tmp = sb("pre_tmp", [P, 2, T])
        rows = sb("rows", [P, T])
        dbc, cwT = rows[0:NX, :], rows[E0:E0 + NE, :]
        h1 = sb("h1", [P, NTB, D])
        mT = sb("mT", [P, KD, T])
        post_tmp = sb("post_tmp", [P, CT, T])
        stats = {k: sb(f"stats_{k}", [P, NTB, 6]) for k in ("pre", "post")}
        mv = {k: sb(f"mv_{k}", [P, NTB, 2]) for k in ("pre", "post")}
        ve = {k: sb(f"ve_{k}", [P, NTB]) for k in ("pre", "post")}
        nb = {k: sb(f"nb_{k}", [P, NTB]) for k in ("pre", "post")}
        rs = {k: sb(f"rs_{k}", [P, NTB]) for k in ("pre", "post")}
        r1 = [sb(f"r1_{i}", [P, NTB]) for i in range(6)]
        r8 = [sb(f"r8_{i}", [P, NTB, NE]) for i in range(6)]

        NA, NH, ND = 2, 2, 4
        ps = [ctx.enter_context(nc.psum_tensor(f"ps{i}", [P, 512], F32)) for i in range(NA + NH + ND)]
        psA, psH, psD = ps[:NA], ps[NA:NA + NH], ps[NA + NH:]
        B_scratch = nc.dram_tensor("B_scratch", (NB, NS * T), F32, kind="Internal").ap()

        free_banks = [(i, None) for i in range(ND)]

        def take_bank():
            i, reader = free_banks.pop(0)
            if reader:
                need("pe", *reader)
            return i, psD[i]

        def give_bank(i, reader):
            free_banks.append((i, reader))

        nloads = [0]

        def bring(dst, src):
            p.load("sp", lambda e: e.dma_start(dst, src), "weights", nloads[0])
            nloads[0] += 1

        def constants():
            bring(norm1[:], a["norm1"])
            bring(w_in[:], a["in_proj_w"])
            for dst, key in ((conv_w, "conv_w"), (conv_b, "conv_b"), (w_x, "x_proj_w"), (w_dt, "dt_proj_w"),
                             (dt_b, "dt_proj_b"), (A, "A_log"), (D_half, "D_param"), (w_out, "out_proj_w"),
                             (norm2, "norm2"), (w_m1, "mlp_w1"), (b1, "mlp_b1"), (w_m2, "mlp_w2"),
                             (w_gate, "gate_w"), (w_g, "wg"), (w_u, "wu"), (w_d, "wd")):
                bring(dst[:], a[key])
            bring(b2[:], a["mlp_b2"].broadcast_to([P, D]))
            last = nloads[0] - 1
            do("pool", lambda e: e.memset(ident[:], 0.0), "zeroed", 0)
            do("pool", lambda e: e.memset(m_half[:], -0.5), "consts", 0)
            for k in range(NE):
                do("pool", lambda e, k=k: e.memset(rank[:, :, k:k + 1], float(NE - k)), "consts", 1 + k)
            need("pool", "zeroed", 0)
            do("pool", lambda e: e.affine_select(out=ident[:], in_=ident[:], compare_op=ALU.not_equal, fill=1.0,
                                                 base=0, pattern=[[-1, P]], channel_multiplier=1),
               "consts", "all")
            need("dve", "weights", last)
            halves = [(w_x[:], 0.5), (w_x[:, :, R:R + NS], 0.5), (w_out[:], 0.5), (w_d[:], 0.5), (D_half[:], 0.5)]
            for k, (w, f) in enumerate(halves):
                if k == 1:
                    need("dve", "halved", 0)
                do("dve", lambda e, w=w, f=f: e.tensor_scalar(w, w, f, None, ALU.mult), "halved", k)
            need("act", "weights", last)
            do("act", lambda e: e.activation(A[:], A[:], ACT.Exp), "A_exp", 0)
            need("dve", "A_exp", 0)
            do("dve", lambda e: e.tensor_scalar(A[:], A[:], -1.0, None, ALU.mult), "halved", "all")
            for e in ("act", "pe", "pool", "dve"):
                need(e, "weights", last)
                need(e, "halved", "all")
                need(e, "consts", "all")

        def ln_stats(k, src, b):
            for i in range(NTB):
                do("dve", lambda e, i=i: e.bn_stats(stats[k][:, i, :], src[:, i, :]), "bn_" + k, (b, i))
            need("dve", "bn_" + k, (b, NTB - 1))
            if ("rstd_" + k, prev_ln[k]) in p.value:
                need("dve", "rstd_" + k, prev_ln[k])
            for i in range(NTB):
                do("dve", lambda e, i=i: e.bn_aggr(mv[k][:, i, :], stats[k][:, i, :]), "mean_" + k, (b, i))
            need("dve", "mean_" + k, (b, NTB - 1))
            do("dve", lambda e: e.tensor_scalar(ve[k][:], mv[k][:, :, 1], EPS, None, ALU.add), "var_" + k, b)
            need("pool", "var_" + k, b)
            if ("norm_" + k, prev_ln[k]) in p.value:
                need("pool", "norm_" + k, prev_ln[k])
            do("pool", lambda e: e.tensor_tensor(rs[k][:], ve[k][:], m_half[:], ALU.pow), "rstd_" + k, b)
            prev_ln[k] = b

        prev_ln = {"pre": None, "post": None}

        def ln_shift(k, b):
            need("dve", "rstd_" + k, b)
            if prev_norm[k] is not None:
                need("dve", "norm_" + k, prev_norm[k])
            do("dve", lambda e: e.scalar_tensor_tensor(out=nb[k][:], in0=mv[k][:, :, 0], scalar=-1.0, in1=rs[k][:],
                                                       op0=ALU.mult, op1=ALU.mult), "shift_" + k, b)

        def ln_apply(k, src, dst, b):
            need("act", "shift_" + k, b)
            for i in range(NTB):
                do("act", lambda e, i=i: e.activation(dst[:, i, :], src[:, i, :], ACT.Identity,
                                                      scale=rs[k][:, i:i + 1], bias=nb[k][:, i:i + 1]),
                   "norm_" + k, b if i == NTB - 1 else (b, i))
            prev_norm[k] = b

        prev_norm = {"pre": None, "post": None}

        def to_channels(src, ready, evict):
            for kt in range(KD):
                i, bank = take_bank()
                need("pe", *ready)
                for t in range(NTB):
                    fn = lambda e, t=t, kt=kt, bank=bank: e.transpose(
                        bank[:, t * P:(t + 1) * P], src[:, t, kt * P:(kt + 1) * P], ident[:])
                    if t == NTB - 1:
                        do("pe", fn, "turned", p.count.get("turned", 0))
                    else:
                        do("pe", fn)
                at = p.count["turned"] - 1
                yield 0.6
                need("act", "turned", at)
                evict(kt, bank, i)

        def scaled_evict(norm, dst, step, b):
            def evict(kt, bank, i):
                do("act", lambda e: e.activation(dst[:, kt, :], bank[:], ACT.Identity, scale=norm[:, 0, kt:kt + 1],
                                                 bias=norm[:, 1, kt:kt + 1]), step, (b, kt))
                give_bank(i, (step, (b, kt)))
            return evict

        def pre(b):
            x, xn, c, s2 = xt[b % 3], xnT[b % 2], xc[b % 2], b % 2
            if b >= 3:
                need("sp", "stored", b - 3)
            p.load("sp", lambda e: e.dma_start(x[:], a["x"][b].rearrange("(t p) d -> p t d", p=P)),
                   "x_in", b, lane=str(b % 3))
            yield 0.5
            need("dve", "x_in", b)
            ln_stats("pre", x, b)
            yield 3.0
            yield 0.1
            tok = pre_tmp[:].rearrange("p a (t d) -> p (a t) d", d=D)
            ln_shift("pre", b)
            yield 0.4
            if b:
                need("act", "dt_sum", (b - 1, CT - 2))
            ln_apply("pre", x, tok, b)
            yield 0.8
            if b >= 2:
                need("act", "z_mm", (b - 2, CT - 1))
            yield from to_channels(tok, ("norm_pre", b), scaled_evict(norm1, xn, "xnT", b))
            yield 0.6
            for j in range(CT):
                i, bank = take_bank()
                need("pe", "xnT", (b, KD - 1))
                for k in range(KD):
                    fn = lambda e, j=j, k=k, bank=bank: e.matmul(
                        bank[:], w_in[:, k, j * P:(j + 1) * P], xn[:, k, :], start=(k == 0), stop=(k == KD - 1))
                    do("pe", fn, *(("in_mm", (b, j)) if k == KD - 1 else ()))
                    yield 0.9
                need("act", "in_mm", (b, j))
                if b >= 2:
                    need("act", "out_mm", (b - 2, 1))
                do("act", lambda e, j=j, bank=bank: e.activation(
                    c[:, j, :], bank[:], ACT.Identity, scale=conv_w[:, j, NK - 1:NK], bias=conv_b[:, j:j + 1]),
                    "tap0", (b, j))
                yield 0.7
                need("dve", "tap0", (b, j))
                for s in range(1, NK):
                    if s > 1:
                        need("dve", "tap", (b, j, s - 1))
                    do("dve", lambda e, j=j, s=s, bank=bank: e.scalar_tensor_tensor(
                        out=c[:, j, s:], in0=bank[:, 0:T - s], scalar=conv_w[:, j, NK - 1 - s:NK - s],
                        in1=c[:, j, s:], op0=ALU.mult, op1=ALU.add), "tap", (b, j, s))
                    if s < NK - 1:
                        yield 0.7
                give_bank(i, ("tap", (b, j, NK - 1)))
                need("act", "tap", (b, j, NK - 1))
                if j >= 2:
                    need("act", "silu_x", (b, j - 2))
                do("act", lambda e, j=j: e.activation(pre_tmp[:, j % 2, :], c[:, j, :], ACT.Tanh, scale=0.5),
                   "tanh_x", (b, j))
                yield 0.9
                need("dve", "tanh_x", (b, j))
                do("dve", lambda e, j=j: e.scalar_tensor_tensor(
                    out=c[:, j, :], in0=pre_tmp[:, j % 2, :], scalar=1.0, in1=c[:, j, :], op0=ALU.add, op1=ALU.mult),
                    "silu_x", (b, j))
                yield 0.7
            i, bank = take_bank()
            need("pe", "silu_x", (b, CT - 1))
            for k in range(CT):
                fn = lambda e, k=k, bank=bank: e.matmul(bank[0:NX, :], w_x[:, k, :], c[:, k, :], start=(k == 0),
                                                        stop=(k == CT - 1))
                do("pe", fn, *(("x_mm", b) if k == CT - 1 else ()))
                yield 0.9
            need("act", "x_mm", b)
            if b:
                need("act", "B_out", b - 1)
            do("act", lambda e, bank=bank: e.activation(dbc, bank[0:NX, :], ACT.Copy), "dbc", b)
            give_bank(i, ("dbc", b))
            need("sp", "dbc", b)
            p.load("sp", lambda e: e.dma_start(B_scratch[b].rearrange("(n t) -> n t", t=T), dbc[R:R + NS, :]),
                   "B_out", b)
            yield 0.6
            i, bank = take_bank()
            need("pe", "dbc", b)
            for t in range(NTB):
                fn = lambda e, t=t, bank=bank: e.transpose(bank[:, t * NS:(t + 1) * NS],
                                                           dbc[R + NS:NX, t * P:(t + 1) * P],
                                                           ident[R + NS:NX, R + NS:NX])
                do("pe", fn, *(("C_turned", b) if t == NTB - 1 else ()))
            need("act", "C_turned", b)
            if b >= 2:
                need("act", "weighed", ((b - 2) * NS + NS - 1) * NTB + NTB - 1)
            do("act", lambda e, bank=bank: e.activation(C_tok[s2][:], bank[:, 0:NTB * NS].rearrange(
                "p (t n) -> p t n", n=NS), ACT.Copy), "C_tok", b)
            give_bank(i, ("C_tok", b))
            for j0 in range(0, CT, 2):
                for j in (j0, j0 + 1):
                    i, bank = take_bank()
                    do("pe", lambda e, j=j, bank=bank: e.matmul(bank[:], w_dt[:, j * P:(j + 1) * P], dbc[0:R, :],
                                                                start=True, stop=True), "dt_mm", (b, j))
                    yield 0.5
                    need("act", "dt_mm", (b, j))
                    need("act", "silu_x", (b, CT - 1))
                    if j0:
                        need("act", "dt_sum", (b, j0 - 2))
                    do("act", lambda e, j=j, bank=bank: e.activation(pre_tmp[:, j % 2, :], bank[:], ACT.Abs,
                                                                     bias=dt_b[:, j:j + 1]), "dt_abs", (b, j))
                    if b >= 2:
                        need("act", "dtx", (b - 2, CT - 2))
                    do("act", lambda e, j=j, bank=bank: e.activation(dt[s2][:, j, :], bank[:], ACT.Relu,
                                                                     bias=dt_b[:, j:j + 1]), "dt_relu", (b, j))
                    give_bank(i, ("dt_relu", (b, j)))
                    yield 0.9
                need("act", "dt_abs", (b, j0 + 1))
                do("act", lambda e: e.activation(pre_tmp[:], pre_tmp[:], ACT.Exp, scale=-1.0), "dt_exp", (b, j0))
                need("act", "dt_exp", (b, j0))
                do("act", lambda e: e.activation(pre_tmp[:], pre_tmp[:], ACT.Ln, bias=1.0), "dt_ln", (b, j0))
                yield 0.9
                two = slice(j0, j0 + 2)
                need("pool", "dt_ln", (b, j0))
                need("pool", "dt_relu", (b, j0 + 1))
                do("pool", lambda e, two=two: e.tensor_tensor(dt[s2][:, two, :], dt[s2][:, two, :], pre_tmp[:],
                                                              ALU.add), "dt_sum", (b, j0))
                need("pool", "dt_sum", (b, j0))
                need("pool", "silu_x", (b, CT - 1))
                do("pool", lambda e, two=two: e.tensor_tensor(dtx[s2][:, two, :], dt[s2][:, two, :], c[:, two, :],
                                                              ALU.mult), "dtx", (b, j0))

        def load_B(g):
            b, ch = divmod(g, NCH)
            if g >= NBB:
                need("sp", "dBx", ((g - NBB) * CH + CH - 1) * 2 + 1)
            need("sp", "B_out", b)
            p.load("sp", lambda e: e.dma_start(
                Bbc[g % NBB][:].rearrange("p n t -> p (n t)"),
                B_scratch[b:b + 1, ch * CH * T:(ch + 1) * CH * T].broadcast_to([P, CH * T])),
                "B_in", g, lane=str(g % NBB))

        def make_dBx(b, n, q):
            g = b * NCH + n // CH
            need("pool", "B_in", g)
            need("pool", "dtx", (b, 2 * q))
            u = (b * NS + n) * 2 + q
            if u >= 3:
                need("pool", "scan", (u - 3) * 2 + 1)
            do("pool", lambda e: e.tensor_tensor(
                dBx[u % 3][:], dtx[b % 2][:, 2 * q:2 * q + 2, :],
                Bbc[g % NBB][:, n % CH:n % CH + 1, :].broadcast_to([P, 2, T]), ALU.mult), "dBx", u)

        def decay(b, n, j):
            s = (b * NS + n) * CT + j
            if s >= NA:
                need("act", "scan", s - NA)
            need("act", "dt_sum", (b, j // 2 * 2))
            do("act", lambda e: e.activation(psA[s % NA][:], dt[b % 2][:, j, :], ACT.Exp, scale=A[:, j, n:n + 1]),
               "dA", s)

        def scan(b, n, j):
            s = (b * NS + n) * CT + j
            need("dve", "dA", s)
            need("dve", "dBx", s // 2)
            if s >= NHB:
                need("dve", "h_turned", (s - NHB) // CT * NTB + NTB - 1)
            do("dve", lambda e: e.tensor_tensor_scan(hs[s % NHB][:], psA[s % NA][:], dBx[s // 2 % 3][:, s % 2, :],
                                                     0.0, ALU.mult, ALU.add), "scan", s)

        def weighed(w):
            return ("weighed0" if w // NTB % NS == 0 else "weighed"), w

        def turn(b, n, t):
            w = (b * NS + n) * NTB + t
            if w >= NH:
                need("pe", *weighed(w - NH))
            need("pe", "scan", (b * NS + n) * CT + CT - 1)
            for j in range(CT):
                s = (b * NS + n) * CT + j
                fn = lambda e, j=j, s=s: e.transpose(psH[w % NH][:, j * P:(j + 1) * P],
                                                     hs[s % NHB][:, t * P:(t + 1) * P], ident[:])
                do("pe", fn, *(("h_turned", w) if j == CT - 1 else ()))

        def weigh(b, n, t):
            w = (b * NS + n) * NTB + t
            o = acc[b % 2][:, t, :]
            if n == 0:
                need("act", "h_turned", w)
                need("act", "C_tok", b)
                if b >= 2:
                    need("act", "y_turned", (b - 2, CT - 1))
                do("act", lambda e: e.activation(o, psH[w % NH][:], ACT.Copy, scale=C_tok[b % 2][:, t, n:n + 1]),
                   "weighed0", w)
            else:
                need("dve", "h_turned", w)
                need("dve", "C_tok", b)
                need("dve", *weighed(w - NTB))
                do("dve", lambda e: e.scalar_tensor_tensor(out=o, in0=psH[w % NH][:],
                                                           scalar=C_tok[b % 2][:, t, n:n + 1], in1=o,
                                                           op0=ALU.mult, op1=ALU.add), "weighed", w)

        def gate_and_project(b):
            x, xn, c = xt[b % 3], xnT[b % 2], xc[b % 2]
            zt = post_tmp
            for j in range(CT):
                i, bank = take_bank()
                for k in range(KD):
                    fn = lambda e, j=j, k=k, bank=bank: e.matmul(
                        bank[:], w_in[:, k, DI + j * P:DI + (j + 1) * P], xn[:, k, :], start=(k == 0),
                        stop=(k == KD - 1))
                    do("pe", fn, *(("z_mm", (b, j)) if k == KD - 1 else ()))
                    yield 0.9
                need("act", "z_mm", (b, j))
                if b:
                    need("act", "down_mm", (b - 1, 2 * NE + 1))
                do("act", lambda e, j=j, bank=bank: e.activation(zt[:, j, :], bank[:], ACT.Tanh, scale=0.5),
                   "tanh_z", (b, j))
                yield 1.0
                need("dve", "tanh_z", (b, j))
                do("dve", lambda e, j=j, bank=bank: e.scalar_tensor_tensor(
                    out=zt[:, j, :], in0=zt[:, j, :], scalar=1.0, in1=bank[:], op0=ALU.add, op1=ALU.mult),
                    "silu_z", (b, j))
                give_bank(i, ("silu_z", (b, j)))
                yield 0.7
                i, bank = take_bank()
                need("pe", "weighed", (b * NS + NS - 1) * NTB + NTB - 1)
                for t in range(NTB):
                    fn = lambda e, j=j, t=t, bank=bank: e.transpose(
                        bank[:, t * P:(t + 1) * P], acc[b % 2][:, t, j * P:(j + 1) * P], ident[:])
                    do("pe", fn, *(("y_turned", (b, j)) if t == NTB - 1 else ()))
                yield 0.5
                need("dve", "y_turned", (b, j))
                do("dve", lambda e, j=j, bank=bank: e.scalar_tensor_tensor(
                    out=c[:, j, :], in0=c[:, j, :], scalar=D_half[:, j:j + 1], in1=bank[:], op0=ALU.mult,
                    op1=ALU.add), "y_plus", (b, j))
                give_bank(i, ("y_plus", (b, j)))
                need("pool", "y_plus", (b, j))
                do("pool", lambda e, j=j: e.tensor_tensor(c[:, j, :], c[:, j, :], zt[:, j, :], ALU.mult),
                   "gated", (b, j))
            yield 0.7
            for q in range(2):
                i, bank = take_bank()
                need("pe", "gated", (b, CT - 1))
                for t in range(2):
                    for k in range(CT):
                        fn = lambda e, q=q, t=t, k=k, bank=bank: e.matmul(
                            bank[:, t * D:(t + 1) * D], c[:, k, (2 * q + t) * P:(2 * q + t + 1) * P], w_out[:, k, :],
                            start=(k == 0), stop=(k == CT - 1))
                        do("pe", fn, *(("out_mm", (b, q)) if (t, k) == (1, CT - 1) else ()))
                        if k % 2:
                            yield 0.9
                need("dve", "out_mm", (b, q))
                do("dve", lambda e, q=q, bank=bank: e.tensor_tensor(
                    h1[:, 2 * q:2 * q + 2, :], bank[:].rearrange("p (t d) -> p t d", d=D), x[:, 2 * q:2 * q + 2, :],
                    ALU.add), "h1", (b, q))
                give_bank(i, ("h1", (b, q)))
                yield 0.7

        def mlp(b):
            x = xt[b % 3]
            need("pool", "h1", (b, 1))
            do("pool", lambda e: e.tensor_tensor(x[:], x[:], h1[:], ALU.add), "x_plus", b)
            need("pool", "x_plus", b)
            do("pool", lambda e: e.tensor_tensor(x[:], x[:], b2[:].rearrange("p (a d) -> p a d", a=1).broadcast_to(
                [P, NTB, D]), ALU.add), "x_plus2", b)
            need("dve", "h1", (b, 1))
            ln_stats("post", h1, (b, 2))
            yield 4.0
            tok = post_tmp[:, 0:2, :].rearrange("p a (t d) -> p (a t) d", d=D)
            ln_shift("post", (b, 2))
            yield 0.4
            need("act", "gated", (b, CT - 1))
            ln_apply("post", h1, tok, (b, 2))
            yield 0.8
            yield from to_channels(tok, ("norm_post", (b, 2)), scaled_evict(norm2, mT, "mT", b))
            yield 0.6
            for j in range(CT):
                i, bank = take_bank()
                need("pe", "mT", (b, KD - 1))
                for k in range(KD):
                    fn = lambda e, j=j, k=k, bank=bank: e.matmul(
                        bank[:], w_m1[:, k, j * P:(j + 1) * P], mT[:, k, :], start=(k == 0), stop=(k == KD - 1))
                    do("pe", fn, *(("m1_mm", (b, j)) if k == KD - 1 else ()))
                    yield 0.9
                need("act", "m1_mm", (b, j))
                do("act", lambda e, j=j, bank=bank: e.activation(post_tmp[:, j, :], bank[:], ACT.Gelu,
                                                                 bias=b1[:, j:j + 1]), "gelu", (b, j))
                give_bank(i, ("gelu", (b, j)))
                yield 0.3
            for q in range(2):
                i, bank = take_bank()
                need("pe", "gelu", (b, CT - 1))
                for t in range(2):
                    for k in range(CT):
                        fn = lambda e, q=q, t=t, k=k, bank=bank: e.matmul(
                            bank[:, t * D:(t + 1) * D], post_tmp[:, k, (2 * q + t) * P:(2 * q + t + 1) * P],
                            w_m2[:, k, :], start=(k == 0), stop=(k == CT - 1))
                        do("pe", fn, *(("m2_mm", (b, q)) if (t, k) == (1, CT - 1) else ()))
                        if k % 2:
                            yield 0.9
                need("dve", "m2_mm", (b, q))
                need("dve", "x_plus2", b)
                do("dve", lambda e, q=q, bank=bank: e.tensor_tensor(
                    x[:, 2 * q:2 * q + 2, :], bank[:].rearrange("p (t d) -> p t d", d=D), x[:, 2 * q:2 * q + 2, :],
                    ALU.add), "r", (b, q))
                give_bank(i, ("r", (b, q)))
                yield 0.7
            need("dve", "r", (b, 1))
            ln_stats("post", x, (b, 3))
            yield 4.0
            ln_shift("post", (b, 3))
            yield 0.4
            ln_apply("post", x, h1, (b, 3))
            yield 0.8

            def plain_evict(kt, bank, i):
                do("act", lambda e: e.activation(mT[:, kt, :], bank[:], ACT.Copy), "x2T", (b, kt))
                give_bank(i, ("x2T", (b, kt)))
            yield from to_channels(h1, ("norm_post", (b, 3)), plain_evict)
            yield 0.6
            i, bank = take_bank()
            need("pe", "x2T", (b, KD - 1))
            for k in range(KD):
                fn = lambda e, k=k, bank=bank: e.matmul(bank[0:NE, :], w_gate[:, k, :], mT[:, k, :],
                                                        start=(k == 0), stop=(k == KD - 1))
                do("pe", fn, *(("gate_mm", b) if k == KD - 1 else ()))
            yield 1.0
            need("act", "gate_mm", b)
            do("act", lambda e, bank=bank: e.activation(cwT, bank[0:NE, :], ACT.Copy), "logits", b)
            give_bank(i, ("logits", b))
            yield 0.3
            i, bank = take_bank()
            need("pe", "logits", b)
            for t in range(NTB):
                fn = lambda e, t=t, bank=bank: e.transpose(bank[:, t * NE:(t + 1) * NE], cwT[:, t * P:(t + 1) * P],
                                                           ident[E0:E0 + NE, E0:E0 + NE])
                do("pe", fn, *(("logits_turned", b) if t == NTB - 1 else ()))
            yield 0.3
            need("dve", "logits_turned", b)
            lg = bank[:, 0:NTB * NE].rearrange("p (t e) -> p t e", e=NE)
            mx, sm, top1, key1, top2, key2 = r1
            pr, eq, key, one1, rest, cw = r8

            def wide(v):
                return v[:].rearrange("p (t o) -> p t o", o=1).broadcast_to([P, NTB, NE])

            nr = [0]

            def route(fn):
                if nr[0]:
                    need("dve", "route", (b, nr[0] - 1))
                do("dve", fn, "route", (b, nr[0]))
                nr[0] += 1

            route(lambda e: e.tensor_reduce(mx[:], lg, AX.X, ALU.max))
            yield 0.1
            route(lambda e: e.tensor_tensor(pr[:], lg, wide(mx), ALU.subtract))
            yield 0.1
            give_bank(i, ("route", (b, nr[0] - 1)))
            need("act", "route", (b, nr[0] - 1))
            do("act", lambda e: e.activation(pr[:], pr[:], ACT.Exp), "route_exp", b)
            yield 0.3
            def router():
                need("dve", "route_exp", b)
                route(lambda e: e.tensor_reduce(sm[:], pr[:], AX.X, ALU.add))
                yield 0.1
                route(lambda e: e.reciprocal(sm[:], sm[:]))
                yield 0.1
                route(lambda e: e.tensor_tensor(pr[:], pr[:], wide(sm), ALU.mult))
                yield 0.1
                route(lambda e: e.tensor_reduce(top1[:], pr[:], AX.X, ALU.max))
                yield 0.1
                route(lambda e: e.tensor_tensor(eq[:], pr[:], wide(top1), ALU.is_equal))
                yield 0.1
                route(lambda e: e.tensor_tensor(key[:], eq[:], rank[:], ALU.mult))
                yield 0.1
                route(lambda e: e.tensor_reduce(key1[:], key[:], AX.X, ALU.max))
                yield 0.1
                route(lambda e: e.tensor_tensor(one1[:], rank[:], wide(key1), ALU.is_equal))
                yield 0.1
                route(lambda e: e.scalar_tensor_tensor(out=rest[:], in0=one1[:], scalar=-2.0, in1=pr[:], op0=ALU.mult,
                                                       op1=ALU.add))
                yield 0.1
                route(lambda e: e.tensor_reduce(top2[:], rest[:], AX.X, ALU.max))
                yield 0.1
                route(lambda e: e.tensor_tensor(eq[:], rest[:], wide(top2), ALU.is_equal))
                yield 0.1
                route(lambda e: e.tensor_tensor(key[:], eq[:], rank[:], ALU.mult))
                yield 0.1
                route(lambda e: e.tensor_reduce(key2[:], key[:], AX.X, ALU.max))
                yield 0.1
                route(lambda e: e.tensor_tensor(eq[:], rank[:], wide(key2), ALU.is_equal))
                yield 0.1
                route(lambda e: e.tensor_tensor(eq[:], eq[:], one1[:], ALU.add))
                yield 0.1
                route(lambda e: e.tensor_tensor(cw[:], eq[:], pr[:], ALU.mult))
                yield 0.1
                i, bank = take_bank()
                need("pe", "route", (b, nr[0] - 1))
                for t in range(NTB):
                    fn = lambda e, t=t, bank=bank: e.transpose(bank[0:NE, t * P:(t + 1) * P], cw[:, t, :], ident[:])
                    do("pe", fn, *(("cw_turned", b) if t == NTB - 1 else ()))
                yield 0.5
                need("act", "cw_turned", b)
                do("act", lambda e, bank=bank: e.activation(cwT, bank[0:NE, :], ACT.Copy), "cwT", b)
                give_bank(i, ("cwT", b))
                yield 0.3

            rankings[b] = router()

        def experts(b):
            x = xt[b % 3]
            NG, UNIT, NU = 4, 3, 2 * (NE + 1)
            order = [NE, *range(NE)]
            gt = [post_tmp[:, 2 + k // 2, (k % 2) * HALF:(k % 2 + 1) * HALF] for k in range(NG)]
            gu, cwb, y = {}, {}, {}

            def half(v):
                return slice(v // (NE + 1) * HALF, (v // (NE + 1) + 1) * HALF)

            def up(v, o):
                if o == 0:
                    gu[v] = take_bank()
                bank, x_, w, ts = gu[v][1], order[v % (NE + 1)], w_u if o else w_g, half(v)
                for k in range(KD):
                    fn = lambda e, k=k: e.matmul(bank[:, o:o + HALF], w[:, k, x_ * P:(x_ + 1) * P], mT[:, k, ts],
                                                 start=(k == 0), stop=(k == KD - 1))
                    do("pe", fn, *(("gu_mm", (b, v)) if (o, k) == (HALF, KD - 1) else ()))

            def gate_tanh(v):
                bank, g = gu[v][1], gt[v % NG]
                need("act", "gu_mm", (b, v))
                if v >= NG:
                    need("act", "down_mm", (b, v - NG))
                do("act", lambda e: e.activation(g, bank[:, 0:HALF], ACT.Tanh, scale=0.5), "tanh_g", (b, v))

            def silu(v):
                bank, g = gu[v][1], gt[v % NG]
                need("dve", "tanh_g", (b, v))
                do("dve", lambda e: e.scalar_tensor_tensor(out=g, in0=g, scalar=1.0, in1=bank[:, 0:HALF],
                                                           op0=ALU.add, op1=ALU.mult), "silu_g", (b, v))

            def hidden(v):
                (i, bank), g = gu.pop(v), gt[v % NG]
                need("dve", "silu_g", (b, v))
                do("dve", lambda e: e.tensor_tensor(g, g, bank[:, HALF:T], ALU.mult), "hidden", (b, v))
                give_bank(i, ("hidden", (b, v)))

            def spread_weight(v):
                if v % (NE + 1) == 0:
                    return
                cwb[v] = take_bank()
                bank, x_, ts = cwb[v][1], order[v % (NE + 1)], half(v)
                need("pe", "cwT", b)
                do("pe", lambda e: e.matmul(bank[:, 0:HALF],
                                            ident[E0:E0 + NE, E0 + x_:E0 + x_ + 1].broadcast_to([NE, P]), cwT[:, ts],
                                            start=True, stop=True), "cw_mm", (b, v))

            def weighted(v):
                if v % (NE + 1) == 0:
                    return
                (i, bank), g = cwb.pop(v), gt[v % NG]
                need("dve", "hidden", (b, v))
                need("dve", "cw_mm", (b, v))
                do("dve", lambda e: e.tensor_tensor(g, g, bank[:, 0:HALF], ALU.mult), "weighted", (b, v))
                give_bank(i, ("weighted", (b, v)))

            def down(v):
                at, q, g = v % (NE + 1), v // (NE + 1), gt[v % NG]
                if at == 0:
                    y[q] = take_bank()
                i, bank = y[q]
                need("pe", "weighted" if at else "hidden", (b, v))
                for t in range(2):
                    fn = lambda e, t=t: e.matmul(bank[:, t * D:(t + 1) * D], g[:, t * P:(t + 1) * P],
                                                 w_d[:, order[at], :], start=(at == 0 and t == 0),
                                                 stop=(at == NE), skip_group_check=True)
                    do("pe", fn, *(("down_mm", (b, v)) if t else ()))

            def total(v):
                q = v // (NE + 1)
                if v % (NE + 1) < NE:
                    return
                i, bank = y[q]
                need("dve", "down_mm", (b, v))
                need("dve", "norm_post", (b, 3))
                do("dve", lambda e: e.tensor_tensor(
                    x[:, 2 * q:2 * q + 2, :], bank[:].rearrange("p (t d) -> p t d", d=D),
                    h1[:, 2 * q:2 * q + 2, :], ALU.add), "r2", (b, q))
                give_bank(i, ("r2", (b, q)))

            stages = [(10, total), (9, down), (7, weighted), (5, hidden), (5, spread_weight), (4, silu),
                      (3, gate_tanh), (1, lambda v: up(v, HALF)), (0, lambda v: up(v, 0))]
            for tick in range(UNIT * (NU - 1) + 11):
                if tick < UNIT + 5:
                    for _ in range(2):
                        next(rankings[b], None)
                if tick == UNIT + 4:
                    yield from rankings[b]
                for at, stage in stages:
                    v, rest = divmod(tick - at, UNIT)
                    if rest == 0 and 0 <= v < NU:
                        stage(v)
                yield 1.0
            need("dve", "r2", (b, 1))
            ln_stats("post", x, (b, 4))
            yield 2.0
            ln_shift("post", (b, 4))
            yield 0.4
            ln_apply("post", x, x, (b, 4))
            need("sp", "norm_post", (b, 4))
            p.load("sp", lambda e: e.dma_start(out[b].rearrange("(t p) d -> p t d", p=P), x[:]), "stored", b,
                   lane=str(b % 3))

        rankings = {}

        class Part:

            def __init__(self, pieces, weight):
                self.pieces, self.weight, self.done = pieces, weight, 0.0

            def to(self, share):
                while self.pieces and (share >= 1.0 or self.done < share * self.weight):
                    w = next(self.pieces, None)
                    if w is None:
                        self.pieces = None
                    else:
                        self.done += w

        constants()
        Part(pre(0), 1.0).to(1.0)
        load_B(0)
        load_B(1)
        make_dBx(0, 0, 0)
        make_dBx(0, 0, 1)
        def place(k):
            return k // (NS * CT), k // CT % NS, k % CT

        last_step = NB * NS * CT - 1
        TURN, LAG = CT, CT + 1

        decay(0, 0, 0)
        STEPS = NS * CT
        SPANS = {gate_and_project: (0, 9, 25.3), mlp: (9, 36, 33.1), pre: (9, 36, 39.9), experts: (36, 64, 65.2)}
        parts = []

        def weave(q):
            for part, first, last in parts:
                if q >= first:
                    part.to((q - first + 0.5) / (last - first))

        for k in range(last_step + 1):
            b, n, j = place(k)
            q = k % STEPS
            if j % 2 == 0 and k + CT <= last_step:
                b_, n_, _ = place(k + CT)
                make_dBx(b_, n_, j // 2)
            if k >= TURN:
                turn(*place(k - TURN))
            scan(b, n, j)
            if k < last_step:
                decay(*place(k + 1))
            if q == LAG:
                for part, _, _ in parts:
                    part.to(1.0)
                parts = [(Part(f(b + 1 if f is pre else b - 1), SPANS[f][2]), *SPANS[f][:2]) for f in SPANS
                         if (b + 1 < NB if f is pre else b > 0)]
            weave((q - LAG) % STEPS)
            if k >= LAG:
                weigh(*place(k - LAG))
            weave((q - LAG) % STEPS + 0.5)
            if n % CH == CH - 1 and j == 1 and (b * NS + n) // CH + 2 < NB * NCH:
                load_B((b * NS + n) // CH + 2)
        for part, _, _ in parts:
            part.to(1.0)
        for k in range(last_step + 1, last_step + 1 + LAG):
            if k - TURN <= last_step:
                turn(*place(k - TURN))
            weigh(*place(k - LAG))
        for f in (gate_and_project, mlp, experts):
            Part(f(NB - 1), 1.0).to(1.0)
        for b in range(max(0, NB - 3), NB):
            need("sp", "stored", b)

        block = ctx.enter_context(nc.Block())

        @block.sync
        def _(eng):
            for f in p.queue["sp"]:
                f(eng)

        @block.gpsimd
        def _(eng):
            for f in p.queue["pool"]:
                f(eng)

        @block.scalar
        def _(eng):
            for f in p.queue["act"]:
                f(eng)

        @block.tensor
        def _(eng):
            for f in p.queue["pe"]:
                f(eng)

        @block.vector
        def _(eng):
            for f in p.queue["dve"]:
                f(eng)


def lay_out(i):
    def tiles(w):
        k, m = w.shape
        return w.reshape(k // 128, 128, m).transpose(1, 0, 2)

    def cols(v):
        return v.reshape(-1, 128).T

    g = {k: np.asarray(v) for k, v in i.items()}
    L = lambda k: g["L0_attn_" + k]
    E = lambda k: g["L0_ffn_" + k]
    wg = np.concatenate([E("wg"), E("sg")[None]]).reshape(-1, 256)
    wu = np.concatenate([E("wu"), E("su")[None]]).reshape(-1, 256)
    wd = np.concatenate([E("wd"), E("sd")[None]])
    return {
        "x": L("x"), "norm1": np.stack([cols(L("norm1_g")), cols(L("norm1_b"))], 1),
        "norm2": np.stack([cols(L("norm2_g")), cols(L("norm2_b"))], 1),
        "in_proj_w": tiles(L("in_proj_w").T), "conv_w": tiles(L("conv_w")[:, 0, :]), "conv_b": cols(L("conv_b")),
        "x_proj_w": tiles(L("x_proj_w").T), "dt_proj_w": L("dt_proj_w").T, "dt_proj_b": cols(L("dt_proj_b")),
        "A_log": tiles(L("A_log")), "D_param": cols(L("D_param")), "out_proj_w": tiles(L("out_proj_w").T),
        "mlp_w1": tiles(L("mlp_w1").T), "mlp_b1": cols(L("mlp_b1")), "mlp_w2": tiles(L("mlp_w2").T),
        "mlp_b2": L("mlp_b2")[None, :], "gate_w": tiles(E("gate_w").T), "wg": tiles(wg.T), "wu": tiles(wu.T),
        "wd": wd.transpose(2, 0, 1),
    }


def kernel(**inputs):
    import concourse.bacc as bacc
    from concourse.bass_utils import run_bass_kernel_spmd

    nc = bacc.Bacc("TRN2", target_bir_lowering=False, num_devices=1)
    arrays, aps = {}, {}
    for name, v in lay_out(inputs).items():
        v = np.ascontiguousarray(v)
        arrays[f"in_{name}"] = v
        aps[name] = nc.dram_tensor(f"in_{name}", v.shape, mybir.dt.from_np(v.dtype), kind="ExternalInput").ap()
    out = nc.dram_tensor("out", aps["x"].shape, mybir.dt.float32, kind="ExternalOutput").ap()
    build(nc, aps, out)
    return run_bass_kernel_spmd(nc, [arrays], core_ids=[0]).results[0]["out"]
```

```python
import numpy as np
import concourse.bass as bass
from concourse import mybir
from contextlib import ExitStack


HOLDS = {
    "scan": 602, "weighed": 663, "weighed0": 571, "tap": 660, "silu_g": 335, "hidden": 335, "weighted": 335,
    "bn_pre": 335, "bn_post": 335, "y_plus": 663, "silu_x": 602, "silu_z": 602, "h1": 602, "r": 602, "r2": 602,
    "route": 100, "mean_pre": 75, "mean_post": 75, "var_pre": 75, "var_post": 75, "shift_pre": 100, "shift_post": 100,
    "dA": 615, "gelu": 560, "norm_pre": 250, "norm_post": 250, "tanh_g": 264, "dt_abs": 571, "dt_relu": 571,
    "dt_exp": 950, "dt_ln": 950, "tap0": 664, "tanh_x": 520, "tanh_z": 478, "xnT": 664, "mT": 664, "x2T": 478,
    "dbc": 478, "C_tok": 200, "logits": 478, "cwT": 478, "route_exp": 200,
    "dBx": 2303, "gated": 1225, "dt_sum": 2303, "dtx": 2303, "x_plus": 2303, "x_plus2": 2303, "rstd_pre": 958,
    "rstd_post": 958,
    "h_turned": 117.0, "y_turned": 107, "turned": 107, "C_turned": 60, "logits_turned": 60, "cw_turned": 107,
    "gu_mm": 427, "down_mm": 427, "cw_mm": 107, "out_mm": 427, "m2_mm": 427, "in_mm": 853, "z_mm": 853,
    "m1_mm": 853, "dt_mm": 853, "x_mm": 853, "gate_mm": 853,
}
TABLE = {"dA": "exp", "dt_exp": "exp", "route_exp": "exp", "tanh_x": "exp", "tanh_z": "exp", "tanh_g": "exp",
         "A_exp": "exp", "dt_ln": "ln", "gelu": "gelu"}
TABLE_LOAD = 1280
SIGNAL = 200
TRANSFER = 2500


class Bank:

    def __getitem__(self, at):
        return self.tensor[at]


class Instruction:

    def __init__(self, engine, build, step, at, by, lane, needs, place):
        self.engine, self.build, self.step, self.at, self.by, self.lane = engine, build, step, at, by, lane
        self.needs, self.place, self.takes, self.gives, self.holds = needs, place, [], [], None


class Program:

    def __init__(self, nc, ctx):
        self.nc, self.ctx = nc, ctx
        self.queue = {e: [] for e in ("pe", "act", "dve", "pool", "sp")}
        self.sems, self.count, self.value, self.waited = {}, {}, {}, {}
        self.strands, self.strand, self.place = {}, None, 0.0
        self.clock, self.ended = dict.fromkeys(self.queue, 0.0), {}
        self.free, self.table = [], None

    def sem(self, name):
        if name not in self.sems:
            self.sems[name] = self.ctx.enter_context(self.nc.semaphore("s_" + name))
            self.count[name] = 0
        return self.sems[name]

    def on(self, strand):
        self.strand = self.strands.setdefault(strand, {e: [] for e in self.queue})
        self.needs = {e: [] for e in self.queue}
        self.taken, self.last = [], None

    def do(self, engine, instruction, step=None, at=None, by=1, lane=""):
        i = Instruction(engine, instruction, step, at, by, lane, self.needs[engine], self.place)
        self.needs[engine] = []
        if engine == "pe":
            i.takes, self.taken = self.taken, []
        self.strand[engine].append(i)
        self.last = i

    def load(self, engine, instruction, step, at, lane=""):
        self.do(engine, instruction, step, at, by=16, lane=lane)

    def need(self, engine, step, at):
        self.needs[engine].append((step, at))

    def take_bank(self):
        bank = Bank()
        self.taken.append(bank)
        return bank

    def give_bank(self, bank, reader):
        assert (self.last.step, self.last.at) == reader
        self.last.gives.append(bank)

    def wait(self, engine, step, at):
        name, v = self.value[step, at]
        if self.waited.get((engine, name), 0) < v:
            self.waited[engine, name] = v
            s = self.sems[name]
            self.queue[engine].append(lambda eng: eng.wait_ge(s, v))

    def put(self, i, start):
        for bank in i.takes:
            bank.tensor, reader = self.free.pop(0)
            if reader:
                self.wait("pe", *reader)
        for n in i.needs:
            self.wait(i.engine, *n)
        end = self.clock[i.engine] = start + i.holds
        self.table = TABLE.get(i.step, self.table)
        if i.step is None:
            self.queue[i.engine].append(i.build)
            return
        name = i.step + i.lane
        s = self.sem(name)
        self.count[name] += i.by
        self.value[i.step, i.at] = (name, self.count[name])
        self.ended[i.step, i.at] = end + SIGNAL + (TRANSFER if i.engine == "sp" else 0)
        self.queue[i.engine].append(lambda eng: i.build(eng).then_inc(s, i.by))
        for bank in i.gives:
            self.free.append((bank.tensor, (i.step, i.at)))

    def ready(self, i):
        at = 0.0
        for n in i.needs:
            if n not in self.ended:
                return None
            at = max(at, self.ended[n])
        if len(i.takes) > len(self.free):
            return None
        for k in range(len(i.takes)):
            if self.free[k][1]:
                at = max(at, self.ended[self.free[k][1]])
        return at

    def merge(self, patience):
        for strand in self.strands.values():
            for line in strand.values():
                holds = 0
                for i in reversed(line):
                    if i.step:
                        holds = HOLDS.get(i.step, 100)
                    i.holds = holds
                line.reverse()
        lines = {e: [s[e] for s in self.strands.values() if s[e]] for e in self.queue}
        while any(lines.values()):
            best = None
            for e, clock in self.clock.items():
                could = []
                for line in lines[e]:
                    i = line[-1]
                    r = self.ready(i)
                    if r is not None:
                        load = TABLE_LOAD if TABLE.get(i.step, self.table) != self.table else 0
                        could.append((max(clock, r) + load, line))
                if could:
                    first = min(c[0] for c in could)
                    start, line = min((c for c in could if c[0] <= first + patience), key=lambda c: c[1][-1].place)
                    if best is None or start < best[0]:
                        best = start, line
            if best is None:
                raise RuntimeError("the strands wait for each other")
            start, line = best
            i = line.pop()
            self.put(i, start)
            if not line:
                lines[i.engine].remove(line)
        self.strands = {}


def build(nc, a, out):
    F32, BF16 = mybir.dt.float32, mybir.dt.bfloat16
    ALU = mybir.AluOpType
    ACT = mybir.ActivationFunctionType
    AX = mybir.AxisListType
    P = 128
    NB, T, D = a["x"].shape
    DI = a["conv_w"].shape[1] * P
    NS = a["A_log"].shape[2]
    NK = a["conv_w"].shape[2]
    NE = a["gate_w"].shape[2]
    NTB, KD, CT = T // P, D // P, DI // P
    R = a["dt_proj_w"].shape[0]
    NX = R + 2 * NS
    E0 = 64
    EPS = 1e-5
    HALF = T // 2
    CH, NBB = 2, 3
    NCH = NS // CH

    ctx = ExitStack()
    with ctx:
        def sb(name, shape, dtype=F32):
            return ctx.enter_context(nc.sbuf_tensor(name, shape, dtype))

        p = Program(nc, ctx)
        do, need = p.do, p.need

        w_in = sb("w_in", [P, KD, 2 * DI])
        w_x = sb("w_x", [P, CT, NX])
        w_dt = sb("w_dt", [R, DI])
        w_out = sb("w_out", [P, CT, D])
        w_m1 = sb("w_m1", [P, KD, a["mlp_w1"].shape[2]])
        w_m2 = sb("w_m2", [P, CT, D])
        w_g = sb("w_g", [P, KD, (NE + 1) * P])
        w_u = sb("w_u", [P, KD, (NE + 1) * P])
        w_d = sb("w_d", [P, NE + 1, D])
        w_gate = sb("w_gate", [P, KD, NE])
        ident = sb("ident", [P, P])
        norm1 = sb("norm1", [P, 2, KD])
        norm2 = sb("norm2", [P, 2, KD])
        conv_w = sb("conv_w", [P, CT, NK])
        conv_b = sb("conv_b", [P, CT])
        dt_b = sb("dt_b", [P, CT])
        A = sb("A", [P, CT, NS])
        D_half = sb("D_half", [P, CT])
        b1 = sb("b1", [P, CT])
        b2 = sb("b2", [P, D])
        rank = sb("rank", [P, NTB, NE])
        m_half = sb("m_half", [P, NTB])

        xt = [sb(f"xt{i}", [P, NTB, D]) for i in range(3)]
        xnT = [sb(f"xnT{i}", [P, KD, T]) for i in range(2)]
        xc = [sb(f"xc{i}", [P, CT, T]) for i in range(2)]
        dt = [sb(f"dt{i}", [P, CT, T]) for i in range(2)]
        dtx = [sb(f"dtx{i}", [P, CT, T]) for i in range(2)]
        acc = [sb(f"acc{i}", [P, NTB, DI]) for i in range(2)]
        Bbc = [sb(f"Bbc{i}", [P, CH, T]) for i in range(NBB)]
        C_tok = [sb(f"C_tok{i}", [P, NTB, NS]) for i in range(2)]
        dBx = [sb(f"dBx{i}", [P, 2, T]) for i in range(3)]
        NHB = 3 * CT - 1
        hs = [sb(f"hs{i}", [P, T]) for i in range(NHB)]
        pre_tmp = sb("pre_tmp", [P, 2, T])
        rows = sb("rows", [P, T])
        dbc, logitsT = rows[0:NX, :], rows[E0:E0 + NE, :]
        W3 = 3 * NE
        parts = sb("parts", [P, NTB, 3, NE], BF16)
        partsT = sb("partsT", [W3, T], BF16)
        ident16 = sb("ident16", [P, P], BF16)
        picks = sb("picks", [W3, NE], BF16)
        h1 = sb("h1", [P, NTB, D])
        mT = sb("mT", [P, KD, T])
        post_tmp = sb("post_tmp", [P, CT, T])
        stats = {k: sb(f"stats_{k}", [P, NTB, 6]) for k in ("pre", "post")}
        mv = {k: sb(f"mv_{k}", [P, NTB, 2]) for k in ("pre", "post")}
        ve = {k: sb(f"ve_{k}", [P, NTB]) for k in ("pre", "post")}
        nb = {k: sb(f"nb_{k}", [P, NTB]) for k in ("pre", "post")}
        rs = {k: sb(f"rs_{k}", [P, NTB]) for k in ("pre", "post")}
        r1 = [sb(f"r1_{i}", [P, NTB]) for i in range(6)]
        r8 = [sb(f"r8_{i}", [P, NTB, NE]) for i in range(6)]

        NA, NH, ND = 2, 2, 4
        ps = [ctx.enter_context(nc.psum_tensor(f"ps{i}", [P, 512], F32)) for i in range(NA + NH + ND)]
        psA, psH, psD = ps[:NA], ps[NA:NA + NH], ps[NA + NH:]
        B_scratch = nc.dram_tensor("B_scratch", (NB, NS * T), F32, kind="Internal").ap()

        p.free = [(bank, None) for bank in psD]
        take_bank, give_bank = p.take_bank, p.give_bank

        nloads = [0]

        def bring(dst, src):
            p.load("sp", lambda e: e.dma_start(dst, src), "weights", nloads[0])
            nloads[0] += 1

        def constants():
            bring(norm1[:], a["norm1"])
            bring(w_in[:], a["in_proj_w"])
            for dst, key in ((conv_w, "conv_w"), (conv_b, "conv_b"), (w_x, "x_proj_w"), (w_dt, "dt_proj_w"),
                             (dt_b, "dt_proj_b"), (A, "A_log"), (D_half, "D_param"), (w_out, "out_proj_w"),
                             (norm2, "norm2"), (w_m1, "mlp_w1"), (b1, "mlp_b1"), (w_m2, "mlp_w2"),
                             (w_gate, "gate_w"), (w_g, "wg"), (w_u, "wu"), (w_d, "wd")):
                bring(dst[:], a[key])
            bring(b2[:], a["mlp_b2"].broadcast_to([P, D]))
            last = nloads[0] - 1
            do("pool", lambda e: e.memset(ident[:], 0.0), "zeroed", 0)
            do("pool", lambda e: e.memset(m_half[:], -0.5), "consts", 0)
            for k in range(NE):
                do("pool", lambda e, k=k: e.memset(rank[:, :, k:k + 1], float(NE - k)), "consts", 1 + k)
            need("pool", "zeroed", 0)
            do("pool", lambda e: e.affine_select(out=ident[:], in_=ident[:], compare_op=ALU.not_equal, fill=1.0,
                                                 base=0, pattern=[[-1, P]], channel_multiplier=1),
               "consts", "all")
            need("dve", "weights", last)
            halves = [(w_x[:], 0.5), (w_x[:, :, R:R + NS], 0.5), (w_out[:], 0.5), (w_d[:], 0.5), (D_half[:], 0.5)]
            for k, (w, f) in enumerate(halves):
                if k == 1:
                    need("dve", "halved", 0)
                do("dve", lambda e, w=w, f=f: e.tensor_scalar(w, w, f, None, ALU.mult), "halved", k)
            need("dve", "consts", "all")
            do("dve", lambda e: e.tensor_scalar(ident16[:], ident[:], 1.0, None, ALU.mult), "halved", "ident16")
            do("dve", lambda e: e.tensor_tensor(picks[:], ident[0:W3, 0:NE], ident[0:W3, NE:2 * NE], ALU.add),
               "halved", "picks")
            need("dve", "halved", "picks")
            do("dve", lambda e: e.tensor_tensor(picks[:], picks[:], ident[0:W3, 2 * NE:W3], ALU.add),
               "halved", "picks3")
            need("act", "weights", last)
            do("act", lambda e: e.activation(A[:], A[:], ACT.Exp), "A_exp", 0)
            need("dve", "A_exp", 0)
            do("dve", lambda e: e.tensor_scalar(A[:], A[:], -1.0, None, ALU.mult), "halved", "all")
            return last

        def ln_stats(k, src, b):
            if prev_ln[k] is not None:
                need("dve", "norm_" + k, prev_ln[k])
            for i in range(NTB):
                do("dve", lambda e, i=i: e.bn_stats(stats[k][:, i, :], src[:, i, :]), "bn_" + k, (b, i))
            need("dve", "bn_" + k, (b, NTB - 1))
            for i in range(NTB):
                do("dve", lambda e, i=i: e.bn_aggr(mv[k][:, i, :], stats[k][:, i, :]), "mean_" + k, (b, i))
            need("dve", "mean_" + k, (b, NTB - 1))
            do("dve", lambda e: e.tensor_scalar(ve[k][:], mv[k][:, :, 1], EPS, None, ALU.add), "var_" + k, b)
            need("pool", "var_" + k, b)
            if prev_ln[k] is not None:
                need("pool", "norm_" + k, prev_ln[k])
            do("pool", lambda e: e.tensor_tensor(rs[k][:], ve[k][:], m_half[:], ALU.pow), "rstd_" + k, b)
            prev_ln[k] = b

        prev_ln = {"pre": None, "post": None}

        def ln_shift(k, b):
            need("dve", "rstd_" + k, b)
            do("dve", lambda e: e.scalar_tensor_tensor(out=nb[k][:], in0=mv[k][:, :, 0], scalar=-1.0, in1=rs[k][:],
                                                       op0=ALU.mult, op1=ALU.mult), "shift_" + k, b)

        def ln_apply(k, src, dst, b):
            need("act", "shift_" + k, b)
            for i in range(NTB):
                do("act", lambda e, i=i: e.activation(dst[:, i, :], src[:, i, :], ACT.Identity,
                                                      scale=rs[k][:, i:i + 1], bias=nb[k][:, i:i + 1]),
                   "norm_" + k, b if i == NTB - 1 else (b, i))

        def to_channels(src, ready, evict):
            for kt in range(KD):
                bank = take_bank()
                need("pe", *ready)
                for t in range(NTB):
                    fn = lambda e, t=t, kt=kt, bank=bank: e.transpose(
                        bank[:, t * P:(t + 1) * P], src[:, t, kt * P:(kt + 1) * P], ident[:])
                    do("pe", fn, *(("turned", (ready, kt)) if t == NTB - 1 else ()))
                yield 0.6
                need("act", "turned", (ready, kt))
                evict(kt, bank)

        def scaled_evict(norm, dst, step, b):
            def evict(kt, bank):
                do("act", lambda e: e.activation(dst[:, kt, :], bank[:], ACT.Identity, scale=norm[:, 0, kt:kt + 1],
                                                 bias=norm[:, 1, kt:kt + 1]), step, (b, kt))
                give_bank(bank, (step, (b, kt)))
            return evict

        def pre(b):
            x, xn, c, s2 = xt[b % 3], xnT[b % 2], xc[b % 2], b % 2
            if b >= 3:
                need("sp", "stored", b - 3)
            p.load("sp", lambda e: e.dma_start(x[:], a["x"][b].rearrange("(t p) d -> p t d", p=P)),
                   "x_in", b, lane=str(b % 3))
            yield 0.5
            need("dve", "x_in", b)
            ln_stats("pre", x, b)
            yield 3.0
            yield 0.1
            tok = pre_tmp[:].rearrange("p a (t d) -> p (a t) d", d=D)
            ln_shift("pre", b)
            yield 0.4
            if b:
                need("act", "dt_sum", (b - 1, CT - 2))
            ln_apply("pre", x, tok, b)
            yield 0.8
            if b >= 2:
                need("pe", "z_mm", (b - 2, CT - 1))
                need("act", "z_mm", (b - 2, CT - 1))
            yield from to_channels(tok, ("norm_pre", b), scaled_evict(norm1, xn, "xnT", b))
            yield 0.6
            for j in range(CT):
                if b >= 2 and j == 0:
                    need("pe", "out_mm", (b - 2, 1))
                bank = take_bank()
                need("pe", "xnT", (b, KD - 1))
                for k in range(KD):
                    fn = lambda e, j=j, k=k, bank=bank: e.matmul(
                        bank[:], w_in[:, k, j * P:(j + 1) * P], xn[:, k, :], start=(k == 0), stop=(k == KD - 1))
                    do("pe", fn, *(("in_mm", (b, j)) if k == KD - 1 else ()))
                    yield 0.9
                need("act", "in_mm", (b, j))
                if b >= 2:
                    need("act", "out_mm", (b - 2, 1))
                do("act", lambda e, j=j, bank=bank: e.activation(
                    c[:, j, :], bank[:], ACT.Identity, scale=conv_w[:, j, NK - 1:NK], bias=conv_b[:, j:j + 1]),
                    "tap0", (b, j))
                yield 0.7
                need("dve", "tap0", (b, j))
                for s in range(1, NK):
                    if s > 1:
                        need("dve", "tap", (b, j, s - 1))
                    do("dve", lambda e, j=j, s=s, bank=bank: e.scalar_tensor_tensor(
                        out=c[:, j, s:], in0=bank[:, 0:T - s], scalar=conv_w[:, j, NK - 1 - s:NK - s],
                        in1=c[:, j, s:], op0=ALU.mult, op1=ALU.add), "tap", (b, j, s))
                    if s < NK - 1:
                        yield 0.7
                give_bank(bank, ("tap", (b, j, NK - 1)))
                need("act", "tap", (b, j, NK - 1))
                if j >= 2:
                    need("act", "silu_x", (b, j - 2))
                do("act", lambda e, j=j: e.activation(pre_tmp[:, j % 2, :], c[:, j, :], ACT.Tanh, scale=0.5),
                   "tanh_x", (b, j))
                yield 0.9
                need("dve", "tanh_x", (b, j))
                do("dve", lambda e, j=j: e.scalar_tensor_tensor(
                    out=c[:, j, :], in0=pre_tmp[:, j % 2, :], scalar=1.0, in1=c[:, j, :], op0=ALU.add, op1=ALU.mult),
                    "silu_x", (b, j))
                yield 0.7
            bank = take_bank()
            need("pe", "silu_x", (b, CT - 1))
            for k in range(CT):
                fn = lambda e, k=k, bank=bank: e.matmul(bank[0:NX, :], w_x[:, k, :], c[:, k, :], start=(k == 0),
                                                        stop=(k == CT - 1))
                do("pe", fn, *(("x_mm", b) if k == CT - 1 else ()))
                yield 0.9
            need("act", "x_mm", b)
            if b:
                need("act", "B_out", b - 1)
            do("act", lambda e, bank=bank: e.activation(dbc, bank[0:NX, :], ACT.Copy), "dbc", b)
            give_bank(bank, ("dbc", b))
            need("sp", "dbc", b)
            p.load("sp", lambda e: e.dma_start(B_scratch[b].rearrange("(n t) -> n t", t=T), dbc[R:R + NS, :]),
                   "B_out", b)
            yield 0.6
            bank = take_bank()
            need("pe", "dbc", b)
            for t in range(NTB):
                fn = lambda e, t=t, bank=bank: e.transpose(bank[:, t * NS:(t + 1) * NS],
                                                           dbc[R + NS:NX, t * P:(t + 1) * P],
                                                           ident[R + NS:NX, R + NS:NX])
                do("pe", fn, *(("C_turned", b) if t == NTB - 1 else ()))
            need("act", "C_turned", b)
            if b >= 2:
                need("act", "weighed", ((b - 2) * NS + NS - 1) * NTB + NTB - 1)
            do("act", lambda e, bank=bank: e.activation(C_tok[s2][:], bank[:, 0:NTB * NS].rearrange(
                "p (t n) -> p t n", n=NS), ACT.Copy), "C_tok", b)
            give_bank(bank, ("C_tok", b))
            for j0 in range(0, CT, 2):
                for j in (j0, j0 + 1):
                    bank = take_bank()
                    do("pe", lambda e, j=j, bank=bank: e.matmul(bank[:], w_dt[:, j * P:(j + 1) * P], dbc[0:R, :],
                                                                start=True, stop=True), "dt_mm", (b, j))
                    yield 0.5
                    need("act", "dt_mm", (b, j))
                    need("act", "silu_x", (b, CT - 1))
                    if j0:
                        need("act", "dt_sum", (b, j0 - 2))
                    do("act", lambda e, j=j, bank=bank: e.activation(pre_tmp[:, j % 2, :], bank[:], ACT.Abs,
                                                                     bias=dt_b[:, j:j + 1]), "dt_abs", (b, j))
                    if b >= 2:
                        need("act", "dtx", (b - 2, CT - 2))
                    do("act", lambda e, j=j, bank=bank: e.activation(dt[s2][:, j, :], bank[:], ACT.Relu,
                                                                     bias=dt_b[:, j:j + 1]), "dt_relu", (b, j))
                    give_bank(bank, ("dt_relu", (b, j)))
                    yield 0.9
                need("act", "dt_abs", (b, j0 + 1))
                do("act", lambda e: e.activation(pre_tmp[:], pre_tmp[:], ACT.Exp, scale=-1.0), "dt_exp", (b, j0))
                need("act", "dt_exp", (b, j0))
                do("act", lambda e: e.activation(pre_tmp[:], pre_tmp[:], ACT.Ln, bias=1.0), "dt_ln", (b, j0))
                yield 0.9
                two = slice(j0, j0 + 2)
                need("pool", "dt_ln", (b, j0))
                need("pool", "dt_relu", (b, j0 + 1))
                do("pool", lambda e, two=two: e.tensor_tensor(dt[s2][:, two, :], dt[s2][:, two, :], pre_tmp[:],
                                                              ALU.add), "dt_sum", (b, j0))
                need("pool", "dt_sum", (b, j0))
                need("pool", "silu_x", (b, CT - 1))
                do("pool", lambda e, two=two: e.tensor_tensor(dtx[s2][:, two, :], dt[s2][:, two, :], c[:, two, :],
                                                              ALU.mult), "dtx", (b, j0))

        def load_B(g):
            b, ch = divmod(g, NCH)
            if g >= NBB:
                need("sp", "dBx", ((g - NBB) * CH + CH - 1) * 2 + 1)
            need("sp", "B_out", b)
            p.load("sp", lambda e: e.dma_start(
                Bbc[g % NBB][:].rearrange("p n t -> p (n t)"),
                B_scratch[b:b + 1, ch * CH * T:(ch + 1) * CH * T].broadcast_to([P, CH * T])),
                "B_in", g, lane=str(g % NBB))

        def make_dBx(b, n, q):
            g = b * NCH + n // CH
            need("pool", "B_in", g)
            need("pool", "dtx", (b, 2 * q))
            u = (b * NS + n) * 2 + q
            if u >= 3:
                need("pool", "scan", (u - 3) * 2 + 1)
            do("pool", lambda e: e.tensor_tensor(
                dBx[u % 3][:], dtx[b % 2][:, 2 * q:2 * q + 2, :],
                Bbc[g % NBB][:, n % CH:n % CH + 1, :].broadcast_to([P, 2, T]), ALU.mult), "dBx", u)

        def decay(b, n, j):
            s = (b * NS + n) * CT + j
            if s >= NA:
                need("act", "scan", s - NA)
            need("act", "dt_sum", (b, j // 2 * 2))
            do("act", lambda e: e.activation(psA[s % NA][:], dt[b % 2][:, j, :], ACT.Exp, scale=A[:, j, n:n + 1]),
               "dA", s)

        def scan(b, n, j):
            s = (b * NS + n) * CT + j
            need("dve", "dA", s)
            need("dve", "dBx", s // 2)
            if s >= NHB:
                need("dve", "h_turned", (s - NHB) // CT * NTB + NTB - 1)
            do("dve", lambda e: e.tensor_tensor_scan(hs[s % NHB][:], psA[s % NA][:], dBx[s // 2 % 3][:, s % 2, :],
                                                     0.0, ALU.mult, ALU.add), "scan", s)

        def weighed(w):
            return ("weighed0" if w // NTB % NS == 0 else "weighed"), w

        def turn(b, n, t):
            w = (b * NS + n) * NTB + t
            if w >= NH:
                need("pe", *weighed(w - NH))
            need("pe", "scan", (b * NS + n) * CT + CT - 1)
            for j in range(CT):
                s = (b * NS + n) * CT + j
                fn = lambda e, j=j, s=s: e.transpose(psH[w % NH][:, j * P:(j + 1) * P],
                                                     hs[s % NHB][:, t * P:(t + 1) * P], ident[:])
                do("pe", fn, *(("h_turned", w) if j == CT - 1 else ()))

        def weigh(b, n, t):
            w = (b * NS + n) * NTB + t
            o = acc[b % 2][:, t, :]
            if n == 0:
                need("act", "h_turned", w)
                need("act", "C_tok", b)
                if b >= 2:
                    need("act", "y_turned", (b - 2, CT - 1))
                do("act", lambda e: e.activation(o, psH[w % NH][:], ACT.Copy, scale=C_tok[b % 2][:, t, n:n + 1]),
                   "weighed0", w)
            else:
                need("dve", "h_turned", w)
                need("dve", "C_tok", b)
                need("dve", *weighed(w - NTB))
                do("dve", lambda e: e.scalar_tensor_tensor(out=o, in0=psH[w % NH][:],
                                                           scalar=C_tok[b % 2][:, t, n:n + 1], in1=o,
                                                           op0=ALU.mult, op1=ALU.add), "weighed", w)

        def gate_and_project(b):
            x, xn, c = xt[b % 3], xnT[b % 2], xc[b % 2]
            zt = post_tmp
            for j in range(CT):
                if b and j == 0:
                    need("pe", "down_mm", (b - 1, 2 * NE + 1))
                need("pe", "xnT", (b, KD - 1))
                bank = take_bank()
                for k in range(KD):
                    fn = lambda e, j=j, k=k, bank=bank: e.matmul(
                        bank[:], w_in[:, k, DI + j * P:DI + (j + 1) * P], xn[:, k, :], start=(k == 0),
                        stop=(k == KD - 1))
                    do("pe", fn, *(("z_mm", (b, j)) if k == KD - 1 else ()))
                    yield 0.9
                need("act", "z_mm", (b, j))
                if b:
                    need("act", "down_mm", (b - 1, 2 * NE + 1))
                do("act", lambda e, j=j, bank=bank: e.activation(zt[:, j, :], bank[:], ACT.Tanh, scale=0.5),
                   "tanh_z", (b, j))
                yield 1.0
                need("dve", "tanh_z", (b, j))
                do("dve", lambda e, j=j, bank=bank: e.scalar_tensor_tensor(
                    out=zt[:, j, :], in0=zt[:, j, :], scalar=1.0, in1=bank[:], op0=ALU.add, op1=ALU.mult),
                    "silu_z", (b, j))
                give_bank(bank, ("silu_z", (b, j)))
                yield 0.7
                bank = take_bank()
                need("pe", "weighed", (b * NS + NS - 1) * NTB + NTB - 1)
                for t in range(NTB):
                    fn = lambda e, j=j, t=t, bank=bank: e.transpose(
                        bank[:, t * P:(t + 1) * P], acc[b % 2][:, t, j * P:(j + 1) * P], ident[:])
                    do("pe", fn, *(("y_turned", (b, j)) if t == NTB - 1 else ()))
                yield 0.5
                need("dve", "y_turned", (b, j))
                do("dve", lambda e, j=j, bank=bank: e.scalar_tensor_tensor(
                    out=c[:, j, :], in0=c[:, j, :], scalar=D_half[:, j:j + 1], in1=bank[:], op0=ALU.mult,
                    op1=ALU.add), "y_plus", (b, j))
                give_bank(bank, ("y_plus", (b, j)))
                need("pool", "y_plus", (b, j))
                do("pool", lambda e, j=j: e.tensor_tensor(c[:, j, :], c[:, j, :], zt[:, j, :], ALU.mult),
                   "gated", (b, j))
            yield 0.7
            for q in range(2):
                bank = take_bank()
                need("pe", "gated", (b, CT - 1))
                for t in range(2):
                    for k in range(CT):
                        fn = lambda e, q=q, t=t, k=k, bank=bank: e.matmul(
                            bank[:, t * D:(t + 1) * D], c[:, k, (2 * q + t) * P:(2 * q + t + 1) * P], w_out[:, k, :],
                            start=(k == 0), stop=(k == CT - 1))
                        do("pe", fn, *(("out_mm", (b, q)) if (t, k) == (1, CT - 1) else ()))
                        if k % 2:
                            yield 0.9
                need("dve", "out_mm", (b, q))
                if b:
                    need("dve", "r2", (b - 1, 1))
                do("dve", lambda e, q=q, bank=bank: e.tensor_tensor(
                    h1[:, 2 * q:2 * q + 2, :], bank[:].rearrange("p (t d) -> p t d", d=D), x[:, 2 * q:2 * q + 2, :],
                    ALU.add), "h1", (b, q))
                give_bank(bank, ("h1", (b, q)))
                yield 0.7

        def mlp(b):
            x = xt[b % 3]
            need("pool", "h1", (b, 1))
            do("pool", lambda e: e.tensor_tensor(x[:], x[:], h1[:], ALU.add), "x_plus", b)
            need("pool", "x_plus", b)
            do("pool", lambda e: e.tensor_tensor(x[:], x[:], b2[:].rearrange("p (a d) -> p a d", a=1).broadcast_to(
                [P, NTB, D]), ALU.add), "x_plus2", b)
            need("dve", "h1", (b, 1))
            ln_stats("post", h1, (b, 2))
            yield 4.0
            tok = post_tmp[:, 0:2, :].rearrange("p a (t d) -> p (a t) d", d=D)
            ln_shift("post", (b, 2))
            yield 0.4
            need("act", "gated", (b, CT - 1))
            ln_apply("post", h1, tok, (b, 2))
            yield 0.8
            yield from to_channels(tok, ("norm_post", (b, 2)), scaled_evict(norm2, mT, "mT", b))
            yield 0.6
            for j in range(CT):
                bank = take_bank()
                need("pe", "mT", (b, KD - 1))
                for k in range(KD):
                    fn = lambda e, j=j, k=k, bank=bank: e.matmul(
                        bank[:], w_m1[:, k, j * P:(j + 1) * P], mT[:, k, :], start=(k == 0), stop=(k == KD - 1))
                    do("pe", fn, *(("m1_mm", (b, j)) if k == KD - 1 else ()))
                    yield 0.9
                need("act", "m1_mm", (b, j))
                do("act", lambda e, j=j, bank=bank: e.activation(post_tmp[:, j, :], bank[:], ACT.Gelu,
                                                                 bias=b1[:, j:j + 1]), "gelu", (b, j))
                give_bank(bank, ("gelu", (b, j)))
                yield 0.3
            for q in range(2):
                bank = take_bank()
                need("pe", "gelu", (b, CT - 1))
                for t in range(2):
                    for k in range(CT):
                        fn = lambda e, q=q, t=t, k=k, bank=bank: e.matmul(
                            bank[:, t * D:(t + 1) * D], post_tmp[:, k, (2 * q + t) * P:(2 * q + t + 1) * P],
                            w_m2[:, k, :], start=(k == 0), stop=(k == CT - 1))
                        do("pe", fn, *(("m2_mm", (b, q)) if (t, k) == (1, CT - 1) else ()))
                        if k % 2:
                            yield 0.9
                need("dve", "m2_mm", (b, q))
                need("dve", "x_plus2", b)
                do("dve", lambda e, q=q, bank=bank: e.tensor_tensor(
                    x[:, 2 * q:2 * q + 2, :], bank[:].rearrange("p (t d) -> p t d", d=D), x[:, 2 * q:2 * q + 2, :],
                    ALU.add), "r", (b, q))
                give_bank(bank, ("r", (b, q)))
                yield 0.7
            need("dve", "r", (b, 1))
            ln_stats("post", x, (b, 3))
            yield 4.0
            ln_shift("post", (b, 3))
            yield 0.4
            ln_apply("post", x, h1, (b, 3))
            yield 0.8

            def plain_evict(kt, bank):
                do("act", lambda e: e.activation(mT[:, kt, :], bank[:], ACT.Copy), "x2T", (b, kt))
                give_bank(bank, ("x2T", (b, kt)))
            yield from to_channels(h1, ("norm_post", (b, 3)), plain_evict)
            yield 0.6
        def router(b):
            bank = take_bank()
            need("pe", "x2T", (b, KD - 1))
            for k in range(KD):
                fn = lambda e, k=k, bank=bank: e.matmul(bank[0:NE, :], w_gate[:, k, :], mT[:, k, :],
                                                        start=(k == 0), stop=(k == KD - 1))
                do("pe", fn, *(("gate_mm", b) if k == KD - 1 else ()))
            yield 1.0
            need("act", "gate_mm", b)
            do("act", lambda e, bank=bank: e.activation(logitsT, bank[0:NE, :], ACT.Copy), "logits", b)
            give_bank(bank, ("logits", b))
            yield 0.3
            bank = take_bank()
            need("pe", "logits", b)
            for t in range(NTB):
                fn = lambda e, t=t, bank=bank: e.transpose(bank[:, t * NE:(t + 1) * NE], logitsT[:, t * P:(t + 1) * P],
                                                           ident[E0:E0 + NE, E0:E0 + NE])
                do("pe", fn, *(("logits_turned", b) if t == NTB - 1 else ()))
            yield 0.3
            need("dve", "logits_turned", b)

            def lg(bank=bank):
                return bank[:, 0:NTB * NE].rearrange("p (t e) -> p t e", e=NE)

            mx, sm, top1, key1, top2, key2 = r1
            pr, eq, key, one1, rest, cw = r8

            def wide(v):
                return v[:].rearrange("p (t o) -> p t o", o=1).broadcast_to([P, NTB, NE])

            nr = [0]

            def route(fn):
                if nr[0]:
                    need("dve", "route", (b, nr[0] - 1))
                do("dve", fn, "route", (b, nr[0]))
                nr[0] += 1

            route(lambda e: e.tensor_reduce(mx[:], lg(), AX.X, ALU.max))
            yield 0.1
            route(lambda e: e.tensor_tensor(pr[:], lg(), wide(mx), ALU.subtract))
            yield 0.1
            give_bank(bank, ("route", (b, nr[0] - 1)))
            need("act", "route", (b, nr[0] - 1))
            do("act", lambda e: e.activation(pr[:], pr[:], ACT.Exp), "route_exp", b)
            yield 0.3
            need("dve", "route_exp", b)
            route(lambda e: e.tensor_reduce(sm[:], pr[:], AX.X, ALU.add))
            yield 0.1
            route(lambda e: e.reciprocal(sm[:], sm[:]))
            yield 0.1
            route(lambda e: e.tensor_tensor(pr[:], pr[:], wide(sm), ALU.mult))
            yield 0.1
            route(lambda e: e.tensor_reduce(top1[:], pr[:], AX.X, ALU.max))
            yield 0.1
            route(lambda e: e.tensor_tensor(eq[:], pr[:], wide(top1), ALU.is_equal))
            yield 0.1
            route(lambda e: e.tensor_tensor(key[:], eq[:], rank[:], ALU.mult))
            yield 0.1
            route(lambda e: e.tensor_reduce(key1[:], key[:], AX.X, ALU.max))
            yield 0.1
            route(lambda e: e.tensor_tensor(one1[:], rank[:], wide(key1), ALU.is_equal))
            yield 0.1
            route(lambda e: e.scalar_tensor_tensor(out=rest[:], in0=one1[:], scalar=-2.0, in1=pr[:], op0=ALU.mult,
                                                   op1=ALU.add))
            yield 0.1
            route(lambda e: e.tensor_reduce(top2[:], rest[:], AX.X, ALU.max))
            yield 0.1
            route(lambda e: e.tensor_tensor(eq[:], rest[:], wide(top2), ALU.is_equal))
            yield 0.1
            route(lambda e: e.tensor_tensor(key[:], eq[:], rank[:], ALU.mult))
            yield 0.1
            route(lambda e: e.tensor_reduce(key2[:], key[:], AX.X, ALU.max))
            yield 0.1
            route(lambda e: e.tensor_tensor(eq[:], rank[:], wide(key2), ALU.is_equal))
            yield 0.1
            route(lambda e: e.tensor_tensor(eq[:], eq[:], one1[:], ALU.add))
            yield 0.1
            route(lambda e: e.tensor_tensor(cw[:], eq[:], pr[:], ALU.mult))
            yield 0.1
            route(lambda e: e.tensor_scalar(parts[:, :, 0, :], cw[:], 1.0, None, ALU.mult))
            route(lambda e: e.tensor_tensor(rest[:], cw[:], parts[:, :, 0, :], ALU.subtract))
            yield 0.1
            route(lambda e: e.tensor_scalar(parts[:, :, 1, :], rest[:], 1.0, None, ALU.mult))
            route(lambda e: e.tensor_tensor(parts[:, :, 2, :], rest[:], parts[:, :, 1, :], ALU.subtract))
            yield 0.1
            bank = take_bank()
            need("pe", "route", (b, nr[0] - 1))
            for t in range(NTB):
                fn = lambda e, t=t, bank=bank: e.matmul(
                    bank[0:W3, t * P:(t + 1) * P], parts[:, t, :, :].rearrange("p s e -> p (s e)"), ident16[:],
                    start=True, stop=True)
                do("pe", fn, *(("cw_turned", b) if t == NTB - 1 else ()))
            yield 0.5
            need("act", "cw_turned", b)
            do("act", lambda e, bank=bank: e.activation(partsT[:], bank[0:W3, :], ACT.Copy), "cwT", b)
            give_bank(bank, ("cwT", b))
            yield 0.3

        def experts(b):
            x = xt[b % 3]
            NG, UNIT, NU = 4, 3, 2 * (NE + 1)
            order = [NE, *range(NE)]
            gt = [post_tmp[:, 2 + k // 2, (k % 2) * HALF:(k % 2 + 1) * HALF] for k in range(NG)]
            gu, cwb, y = {}, {}, {}

            def half(v):
                return slice(v // (NE + 1) * HALF, (v // (NE + 1) + 1) * HALF)

            def up(v, o):
                if o == 0:
                    need("pe", "x2T", (b, KD - 1))
                    if v >= 2:
                        need("pe", "cwT", b)
                    gu[v] = take_bank()
                bank, x_, w, ts = gu[v], order[v % (NE + 1)], w_u if o else w_g, half(v)
                for k in range(KD):
                    fn = lambda e, k=k: e.matmul(bank[:, o:o + HALF], w[:, k, x_ * P:(x_ + 1) * P], mT[:, k, ts],
                                                 start=(k == 0), stop=(k == KD - 1))
                    do("pe", fn, *(("gu_mm", (b, v)) if (o, k) == (HALF, KD - 1) else ()))

            def gate_tanh(v):
                bank, g = gu[v], gt[v % NG]
                need("act", "gu_mm", (b, v))
                if v >= NG:
                    need("act", "down_mm", (b, v - NG))
                do("act", lambda e: e.activation(g, bank[:, 0:HALF], ACT.Tanh, scale=0.5), "tanh_g", (b, v))

            def silu(v):
                bank, g = gu[v], gt[v % NG]
                need("dve", "tanh_g", (b, v))
                do("dve", lambda e: e.scalar_tensor_tensor(out=g, in0=g, scalar=1.0, in1=bank[:, 0:HALF],
                                                           op0=ALU.add, op1=ALU.mult), "silu_g", (b, v))

            def hidden(v):
                bank, g = gu.pop(v), gt[v % NG]
                need("dve", "silu_g", (b, v))
                do("dve", lambda e: e.tensor_tensor(g, g, bank[:, HALF:T], ALU.mult), "hidden", (b, v))
                give_bank(bank, ("hidden", (b, v)))

            def spread_weight(v):
                if v % (NE + 1) == 0:
                    return
                cwb[v] = take_bank()
                bank, x_, ts = cwb[v], order[v % (NE + 1)], half(v)
                need("pe", "cwT", b)
                do("pe", lambda e: e.matmul(bank[:, 0:HALF], picks[:, x_:x_ + 1].broadcast_to([W3, P]),
                                            partsT[:, ts], start=True, stop=True), "cw_mm", (b, v))

            def weighted(v):
                if v % (NE + 1) == 0:
                    return
                bank, g = cwb.pop(v), gt[v % NG]
                need("dve", "hidden", (b, v))
                need("dve", "cw_mm", (b, v))
                do("dve", lambda e: e.tensor_tensor(g, g, bank[:, 0:HALF], ALU.mult), "weighted", (b, v))
                give_bank(bank, ("weighted", (b, v)))

            def down(v):
                at, q, g = v % (NE + 1), v // (NE + 1), gt[v % NG]
                if at == 0:
                    y[q] = take_bank()
                bank = y[q]
                need("pe", "weighted" if at else "hidden", (b, v))
                for t in range(2):
                    fn = lambda e, t=t: e.matmul(bank[:, t * D:(t + 1) * D], g[:, t * P:(t + 1) * P],
                                                 w_d[:, order[at], :], start=(at == 0 and t == 0),
                                                 stop=(at == NE), skip_group_check=True)
                    do("pe", fn, *(("down_mm", (b, v)) if t else ()))

            def total(v):
                q = v // (NE + 1)
                if v % (NE + 1) < NE:
                    return
                bank = y[q]
                need("dve", "down_mm", (b, v))
                need("dve", "norm_post", (b, 3))
                do("dve", lambda e: e.tensor_tensor(
                    x[:, 2 * q:2 * q + 2, :], bank[:].rearrange("p (t d) -> p t d", d=D),
                    h1[:, 2 * q:2 * q + 2, :], ALU.add), "r2", (b, q))
                give_bank(bank, ("r2", (b, q)))

            stages = [(10, total), (9, down), (7, weighted), (5, hidden), (5, spread_weight), (4, silu),
                      (3, gate_tanh), (1, lambda v: up(v, HALF)), (0, lambda v: up(v, 0))]
            for tick in range(UNIT * (NU - 1) + 11):
                for at, stage in stages:
                    v, rest = divmod(tick - at, UNIT)
                    if rest == 0 and 0 <= v < NU:
                        stage(v)
                yield 1.0
            need("dve", "r2", (b, 1))
            ln_stats("post", x, (b, 4))
            yield 2.0
            ln_shift("post", (b, 4))
            yield 0.4
            ln_apply("post", x, x, (b, 4))
            need("sp", "norm_post", (b, 4))
            p.load("sp", lambda e: e.dma_start(out[b].rearrange("(t p) d -> p t d", p=P), x[:]), "stored", b,
                   lane=str(b % 3))

        p.on("start")
        last = constants()
        p.merge(0)
        for e in ("act", "pe", "pool", "dve"):
            p.wait(e, "weights", last)
            p.wait(e, "halved", "all")
            p.wait(e, "consts", "all")
        STEPS = NS * CT
        GATE, MLP, ROUTER, EXPERTS, PRE = (2, 8), (8, 36), (36, 38), (36, 78), (-12, 58)
        EARLY, PATIENCE = 1, 50

        def part(strand, pieces, first, last):
            p.on(strand)
            p.place, before = 0.0, {e: len(line) for e, line in p.strand.items()}
            for weight in pieces:
                p.place += weight
            for e, line in p.strand.items():
                for i in line[before[e]:]:
                    i.place = first + (last - first) * i.place / p.place

        for b in range(NB):
            part("pre", pre(b), (b - 1) * STEPS + PRE[0], (b - 1) * STEPS + PRE[1])
            p.on("scan")
            for k in range(STEPS):
                n, j = divmod(k, CT)
                p.place = b * STEPS + k - EARLY
                if n % CH == 0 and j == 0:
                    load_B((b * NS + n) // CH)
                if j % 2 == 0:
                    make_dBx(b, n, j // 2)
                decay(b, n, j)
                scan(b, n, j)
            p.on("weigh")
            for k in range(STEPS):
                n, t = divmod(k, CT)
                p.place = b * STEPS + k + CT
                turn(b, n, t)
                weigh(b, n, t)
            after = (b + 1) * STEPS
            part("gate", gate_and_project(b), after + GATE[0], after + GATE[1])
            part("mlp", mlp(b), after + MLP[0], after + MLP[1])
            part("router", router(b), after + ROUTER[0], after + ROUTER[1])
            part("experts", experts(b), after + EXPERTS[0], after + EXPERTS[1])
        p.merge(PATIENCE)
        for b in range(max(0, NB - 3), NB):
            p.wait("sp", "stored", b)

        block = ctx.enter_context(nc.Block())

        @block.sync
        def _(eng):
            for f in p.queue["sp"]:
                f(eng)

        @block.gpsimd
        def _(eng):
            for f in p.queue["pool"]:
                f(eng)

        @block.scalar
        def _(eng):
            for f in p.queue["act"]:
                f(eng)

        @block.tensor
        def _(eng):
            for f in p.queue["pe"]:
                f(eng)

        @block.vector
        def _(eng):
            for f in p.queue["dve"]:
                f(eng)


def lay_out(i):
    def tiles(w):
        k, m = w.shape
        return w.reshape(k // 128, 128, m).transpose(1, 0, 2)

    def cols(v):
        return v.reshape(-1, 128).T

    g = {k: np.asarray(v) for k, v in i.items()}
    L = lambda k: g["L0_attn_" + k]
    E = lambda k: g["L0_ffn_" + k]
    wg = np.concatenate([E("wg"), E("sg")[None]]).reshape(-1, 256)
    wu = np.concatenate([E("wu"), E("su")[None]]).reshape(-1, 256)
    wd = np.concatenate([E("wd"), E("sd")[None]])
    return {
        "x": L("x"), "norm1": np.stack([cols(L("norm1_g")), cols(L("norm1_b"))], 1),
        "norm2": np.stack([cols(L("norm2_g")), cols(L("norm2_b"))], 1),
        "in_proj_w": tiles(L("in_proj_w").T), "conv_w": tiles(L("conv_w")[:, 0, :]), "conv_b": cols(L("conv_b")),
        "x_proj_w": tiles(L("x_proj_w").T), "dt_proj_w": L("dt_proj_w").T, "dt_proj_b": cols(L("dt_proj_b")),
        "A_log": tiles(L("A_log")), "D_param": cols(L("D_param")), "out_proj_w": tiles(L("out_proj_w").T),
        "mlp_w1": tiles(L("mlp_w1").T), "mlp_b1": cols(L("mlp_b1")), "mlp_w2": tiles(L("mlp_w2").T),
        "mlp_b2": L("mlp_b2")[None, :], "gate_w": tiles(E("gate_w").T), "wg": tiles(wg.T), "wu": tiles(wu.T),
        "wd": wd.transpose(2, 0, 1),
    }


def kernel(**inputs):
    import concourse.bacc as bacc
    from concourse.bass_utils import run_bass_kernel_spmd

    nc = bacc.Bacc("TRN2", target_bir_lowering=False, num_devices=1)
    arrays, aps = {}, {}
    for name, v in lay_out(inputs).items():
        v = np.ascontiguousarray(v)
        arrays[f"in_{name}"] = v
        aps[name] = nc.dram_tensor(f"in_{name}", v.shape, mybir.dt.from_np(v.dtype), kind="ExternalInput").ap()
    out = nc.dram_tensor("out", aps["x"].shape, mybir.dt.float32, kind="ExternalOutput").ap()
    build(nc, aps, out)
    return run_bass_kernel_spmd(nc, [arrays], core_ids=[0]).results[0]["out"]
```
